# Optimizing a Trainium2 kernel written in Bass

```python
import numpy as np
import jax
import jax.numpy as jnp

def _softmax(x, axis=-1):
    return jax.nn.softmax(x, axis=axis)

def _gelu(x):
    return jax.nn.gelu(x, approximate=True)

def _silu(x):
    return jax.nn.silu(x)

def _sigmoid(x):
    return jax.nn.sigmoid(x)

def _layernorm(x, axis=-1, eps=1e-05):
    m = jnp.mean(x, axis=axis, keepdims=True)
    v = jnp.var(x, axis=axis, keepdims=True)
    return (x - m) / jnp.sqrt(v + eps)

def _scatter_add(tgt, idx, src, axis=0):
    return tgt.at[idx].add(src)

def _segment_sum(src, seg, n):
    return jax.ops.segment_sum(src, seg, n)
kernel_name = 'mk_perceiver_d2_seqx_r4_927892'

def setup_inputs(seed: int=0):
    np.random.seed(seed)
    _w = jnp.asarray

    def _rec_inputs():
        import jax
        import jax.numpy as jnp
        _rk = jax.random.key(seed)
        x = -0.0005146 + 1 * jax.random.normal(jax.random.fold_in(_rk, 1), (32, 64, 256), jnp.float32)
        _lenS = 64 - jax.random.randint(jax.random.fold_in(_rk, 7), (32,), 0, max(1, 64 // 4) + 1, jnp.int32)
        _lenS2 = 1601 - jax.random.randint(jax.random.fold_in(_rk, 8), (32,), 0, max(1, 1601 // 4) + 1, jnp.int32)
        _ctx_768P = jax.random.normal(jax.random.fold_in(_rk, 11), (32, 16, 192), jnp.float32)
        _ctx_768c = jax.random.dirichlet(jax.random.fold_in(_rk, 511), 0.3 * jnp.ones((16,), jnp.float32), (32, 1601))
        _ctx_768t = jnp.einsum('bsk,bkd->bsd', _ctx_768c, _ctx_768P)
        _ctx_768t = _ctx_768t * jax.lax.rsqrt(jnp.mean(jnp.square(_ctx_768t)) + 1e-12) * 0.953939
        ctx_768 = -0.00040386 + 0.999972 * (_ctx_768t + 0.3 * jax.random.normal(jax.random.fold_in(_rk, 611), (32, 1601, 192), jnp.float32))
        _validS = jnp.arange(64)[None, :] < _lenS[:, None]
        _validS2 = jnp.arange(1601)[None, :] < _lenS2[:, None]
        _causal = jnp.tril(jnp.ones((64, 64), dtype=bool))
        mask_BxS2_bk0 = jnp.logical_not(jnp.broadcast_to(_validS2[:, :], (32, 1601)))
        mask_BxS2_bf1 = jnp.ones((32, 1601), dtype=bool)
        return (x, ctx_768, mask_BxS2_bk0, mask_BxS2_bf1)
    x, ctx_768, mask_BxS2_bk0, mask_BxS2_bf1 = _rec_inputs()

    def _L0_xattn_setup():
        import jax, jax.numpy as jnp
        import numpy as np
        DIM_IN, DIM_LAT, DIM_HEAD = (192, 256, 64)
        INNER = max(DIM_LAT, DIM_IN)
        HEADS = INNER // DIM_HEAD
        SCALE = DIM_HEAD ** (-0.5)
        RMS_EPS = 1e-08
        LN_EPS = 1e-05

        def layernorm(x, g, b):
            mu = jnp.mean(x, axis=-1, keepdims=True)
            var = jnp.mean((x - mu) ** 2, axis=-1, keepdims=True)
            return (x - mu) * jax.lax.rsqrt(var + LN_EPS) * g + b

        def rmsnorm(x, gamma):
            norm = jnp.sqrt(jnp.sum(x * x, axis=-1, keepdims=True)) * x.shape[-1] ** (-0.5)
            return x / jnp.maximum(norm, RMS_EPS) * gamma
        key = jax.random.key(seed)
        ks = jax.random.split(key, 12)
        b, n, m = (4, 1024, 128)
        x = jax.random.normal(ks[0], (b, n, DIM_IN), jnp.float32)
        latents = jax.random.normal(ks[1], (b, m, DIM_LAT), jnp.float32)
        mask = jax.random.randint(ks[2], (b, n), 0, 2).astype(bool)
        s = lambda k, sh, fan: jax.random.normal(k, sh, jnp.float32) * fan ** (-0.5)
        return {'x': x, 'latents': latents, 'mask': mask, 'ln_x_g': jnp.ones((DIM_IN,), jnp.float32), 'ln_x_b': jnp.zeros((DIM_IN,), jnp.float32), 'ln_l_g': jnp.ones((DIM_LAT,), jnp.float32), 'ln_l_b': jnp.zeros((DIM_LAT,), jnp.float32), 'qn_g': jnp.ones((DIM_HEAD,), jnp.float32), 'kn_g': jnp.ones((DIM_HEAD,), jnp.float32), 'Wq': s(ks[3], (INNER, DIM_LAT), DIM_LAT), 'Wkv': s(ks[4], (2 * INNER, DIM_IN), DIM_IN), 'Wlkv': s(ks[5], (2 * INNER, DIM_LAT), DIM_LAT), 'Wo': s(ks[6], (DIM_LAT, INNER), INNER), 'bo': jnp.zeros((DIM_LAT,), jnp.float32)}
    _L0_xattn_all = _L0_xattn_setup()
    _L0_xattn_in = {k: v for k, v in _L0_xattn_all.items() if k in ('ln_x_g', 'ln_x_b', 'ln_l_g', 'ln_l_b', 'qn_g', 'kn_g', 'Wq', 'Wkv', 'Wlkv', 'Wo', 'bo')}
    del _L0_xattn_all

    def _L0_attn_setup():
        import jax, jax.numpy as jnp
        import numpy as np
        EMBED = 256
        HEADS = 16
        HDIM = EMBED // HEADS
        B, S = (4, 1024)
        key = jax.random.key(seed)
        ks = jax.random.split(key, 11)
        scale = 1.0 / np.sqrt(EMBED)

        def lin(k):
            return jax.random.uniform(k, (EMBED, EMBED), jnp.float32, -scale, scale)

        def bias(k):
            return jax.random.uniform(k, (EMBED,), jnp.float32, -scale, scale)
        return {'x': jax.random.normal(ks[0], (B, S, EMBED), jnp.float32), 'Wq': lin(ks[1]), 'bq': bias(ks[2]), 'Wk': lin(ks[3]), 'bk': bias(ks[4]), 'Wv': lin(ks[5]), 'bv': bias(ks[6]), 'Wg': lin(ks[7]), 'bg': bias(ks[8]), 'Wo': lin(ks[9]), 'bo': bias(ks[10])}
    _L0_attn_all = _L0_attn_setup()
    _L0_attn_in = {k: v for k, v in _L0_attn_all.items() if k in ('Wq', 'bq', 'Wk', 'bk', 'Wv', 'bv', 'Wg', 'bg', 'Wo', 'bo')}
    del _L0_attn_all

    def _L0_ffn_setup():
        import jax, jax.numpy as jnp
        import numpy as np
        B, S, D_MODEL, D_HIDDEN = (4, 512, 256, 1024)

        def act_quant(x):
            scale = 127.0 / jnp.clip(jnp.max(jnp.abs(x), axis=-1, keepdims=True), 1e-05)
            return jnp.clip(jnp.round(x * scale), -128, 127) / scale

        def weight_quant(w):
            scale = 1.0 / jnp.clip(jnp.mean(jnp.abs(w)), 1e-05)
            return jnp.clip(jnp.round(w * scale), -1, 1) / scale

        def bit_linear(x, w):
            xq = x + jax.lax.stop_gradient(act_quant(x) - x)
            wq = w + jax.lax.stop_gradient(weight_quant(w) - w)
            return jnp.einsum('bsd,hd->bsh', xq, wq)

        def depthwise_conv1d(x_bcl, w, b):
            y = jax.lax.conv_general_dilated(x_bcl, w, window_strides=(1,), padding=[(1, 1)], dimension_numbers=('NCH', 'OIH', 'NCH'), feature_group_count=x_bcl.shape[1])
            return y + b[None, :, None]
        key = jax.random.key(seed)
        ks = jax.random.split(key, 5)
        lim1 = 1.0 / np.sqrt(D_MODEL)
        lim2 = 1.0 / np.sqrt(D_HIDDEN)
        limc = 1.0 / np.sqrt(3.0)
        return {'x': jax.random.normal(ks[0], (B, S, D_MODEL), dtype=jnp.float32), 'w1': jax.random.uniform(ks[1], (D_HIDDEN, D_MODEL), jnp.float32, -lim1, lim1), 'conv_w': jax.random.uniform(ks[2], (D_HIDDEN, 1, 3), jnp.float32, -limc, limc), 'conv_b': jax.random.uniform(ks[3], (D_HIDDEN,), jnp.float32, -limc, limc), 'w2': jax.random.uniform(ks[4], (D_MODEL, D_HIDDEN), jnp.float32, -lim2, lim2)}
    _L0_ffn_all = _L0_ffn_setup()
    _L0_ffn_in = {k: v for k, v in _L0_ffn_all.items() if k in ('w1', 'conv_w', 'conv_b', 'w2')}
    del _L0_ffn_all

    def _L1_xattn_setup():
        import jax, jax.numpy as jnp
        import numpy as np
        DIM = 256
        CTX_DIM = 192
        HEADS = 16
        key = jax.random.key(seed)
        ks = jax.random.split(key, 7)
        B, N, M = (4, 1024, 64)
        x = jax.random.normal(ks[0], (B, N, DIM), dtype=jnp.float32)
        context = jax.random.normal(ks[1], (B, M, CTX_DIM), dtype=jnp.float32)
        context_mask = jnp.ones((B, M), dtype=bool)
        s_d = 1.0 / np.sqrt(DIM)
        s_c = 1.0 / np.sqrt(CTX_DIM)
        Wq = jax.random.normal(ks[2], (DIM, DIM), dtype=jnp.float32) * s_d
        Wk = jax.random.normal(ks[3], (CTX_DIM, DIM), dtype=jnp.float32) * s_c
        Wv = jax.random.normal(ks[4], (CTX_DIM, DIM), dtype=jnp.float32) * s_c
        Wo = jax.random.normal(ks[5], (DIM, DIM), dtype=jnp.float32) * s_d
        return {'x': x, 'context': context, 'context_mask': context_mask, 'Wq': Wq, 'Wk': Wk, 'Wv': Wv, 'Wo': Wo}
    _L1_xattn_all = _L1_xattn_setup()
    _L1_xattn_in = {k: v for k, v in _L1_xattn_all.items() if k in ('Wq', 'Wk', 'Wv', 'Wo')}
    del _L1_xattn_all

    def _L1_attn_setup():
        import math
        import jax, jax.numpy as jnp
        import numpy as np
        DIM = 256
        DIM_QK = 128
        DIM_V = 256
        NUM_BUCKETS = 32
        MAX_DISTANCE = 128

        def _rel_pos_bucket_causal(seq_len):
            q = np.arange(seq_len)
            n = np.maximum(q[:, None] - q[None, :], 0)
            max_exact = NUM_BUCKETS // 2
            is_small = n < max_exact
            nf = np.maximum(n, 1).astype(np.float32)
            val_if_large = max_exact + (np.log(nf / max_exact) / math.log(MAX_DISTANCE / max_exact) * (NUM_BUCKETS - max_exact)).astype(np.int32)
            val_if_large = np.minimum(val_if_large, NUM_BUCKETS - 1)
            return jnp.asarray(np.where(is_small, n, val_if_large), dtype=jnp.int32)

        def laplacian_attn_fn(x):
            mu = math.sqrt(0.5)
            std = math.sqrt(0.25 * math.pi)
            return (1.0 + jax.lax.erf((x - mu) / (std * math.sqrt(2.0)))) * 0.5
        key = jax.random.key(seed)
        ks = jax.random.split(key, 8)
        B, S = (8, 512)
        x = jax.random.normal(ks[0], (B, S, DIM), dtype=jnp.float32)
        Wqk = jax.random.normal(ks[1], (DIM, DIM_QK), dtype=jnp.float32) * (1.0 / math.sqrt(DIM))
        bqk = jnp.zeros((DIM_QK,), dtype=jnp.float32)
        gamma = jax.random.normal(ks[2], (2, DIM_QK), dtype=jnp.float32) * 0.02
        beta = jnp.zeros((2, DIM_QK), dtype=jnp.float32)
        Wv = jax.random.normal(ks[3], (DIM, DIM_V), dtype=jnp.float32) * (1.0 / math.sqrt(DIM))
        bv = jnp.zeros((DIM_V,), dtype=jnp.float32)
        rel_emb = jax.random.normal(ks[4], (NUM_BUCKETS, 1), dtype=jnp.float32) * 0.02
        return {'x': x, 'Wqk': Wqk, 'bqk': bqk, 'gamma': gamma, 'beta': beta, 'Wv': Wv, 'bv': bv, 'rel_emb': rel_emb}
    _L1_attn_all = _L1_attn_setup()
    _L1_attn_in = {k: v for k, v in _L1_attn_all.items() if k in ('Wqk', 'bqk', 'gamma', 'beta', 'Wv', 'bv', 'rel_emb')}
    del _L1_attn_all

    def _L1_ffn_setup():
        import jax, jax.numpy as jnp
        import numpy as np
        CAPACITY_FACTOR = 1.25
        key = jax.random.key(seed)
        k1, k2, k3, k4 = jax.random.split(key, 4)
        B, T, D, F, E = (4, 1024, 256, 1024, 8)
        s = 0.02
        return {'x': jax.random.normal(k1, (B, T, D), dtype=jnp.float32), 'wg': jax.random.normal(k2, (D, E), dtype=jnp.float32) * s, 'W1': jax.random.normal(k3, (E, D, F), dtype=jnp.float32) * s, 'b1': jnp.zeros((E, F), dtype=jnp.float32), 'W2': jax.random.normal(k4, (E, F, D), dtype=jnp.float32) * s, 'b2': jnp.zeros((E, D), dtype=jnp.float32)}
    _L1_ffn_all = _L1_ffn_setup()
    _L1_ffn_in = {k: v for k, v in _L1_ffn_all.items() if k in ('wg', 'W1', 'b1', 'W2', 'b2')}
    del _L1_ffn_all
    return {'x': x, 'ctx_768': ctx_768, 'mask_BxS2_bk0': mask_BxS2_bk0, 'mask_BxS2_bf1': mask_BxS2_bf1, 'L0_xattn_ln_x_g': _L0_xattn_in['ln_x_g'], 'L0_xattn_ln_x_b': _L0_xattn_in['ln_x_b'], 'L0_xattn_ln_l_g': _L0_xattn_in['ln_l_g'], 'L0_xattn_ln_l_b': _L0_xattn_in['ln_l_b'], 'L0_xattn_qn_g': _L0_xattn_in['qn_g'], 'L0_xattn_kn_g': _L0_xattn_in['kn_g'], 'L0_xattn_Wq': _L0_xattn_in['Wq'], 'L0_xattn_Wkv': _L0_xattn_in['Wkv'], 'L0_xattn_Wlkv': _L0_xattn_in['Wlkv'], 'L0_xattn_Wo': _L0_xattn_in['Wo'], 'L0_xattn_bo': _L0_xattn_in['bo'], 'L0_attn_Wq': _L0_attn_in['Wq'], 'L0_attn_bq': _L0_attn_in['bq'], 'L0_attn_Wk': _L0_attn_in['Wk'], 'L0_attn_bk': _L0_attn_in['bk'], 'L0_attn_Wv': _L0_attn_in['Wv'], 'L0_attn_bv': _L0_attn_in['bv'], 'L0_attn_Wg': _L0_attn_in['Wg'], 'L0_attn_bg': _L0_attn_in['bg'], 'L0_attn_Wo': _L0_attn_in['Wo'], 'L0_attn_bo': _L0_attn_in['bo'], 'L0_ffn_w1': _L0_ffn_in['w1'], 'L0_ffn_conv_w': _L0_ffn_in['conv_w'], 'L0_ffn_conv_b': _L0_ffn_in['conv_b'], 'L0_ffn_w2': _L0_ffn_in['w2'], 'L1_xattn_Wq': _L1_xattn_in['Wq'], 'L1_xattn_Wk': _L1_xattn_in['Wk'], 'L1_xattn_Wv': _L1_xattn_in['Wv'], 'L1_xattn_Wo': _L1_xattn_in['Wo'], 'L1_attn_Wqk': _L1_attn_in['Wqk'], 'L1_attn_bqk': _L1_attn_in['bqk'], 'L1_attn_gamma': _L1_attn_in['gamma'], 'L1_attn_beta': _L1_attn_in['beta'], 'L1_attn_Wv': _L1_attn_in['Wv'], 'L1_attn_bv': _L1_attn_in['bv'], 'L1_attn_rel_emb': _L1_attn_in['rel_emb'], 'L1_ffn_wg': _L1_ffn_in['wg'], 'L1_ffn_W1': _L1_ffn_in['W1'], 'L1_ffn_b1': _L1_ffn_in['b1'], 'L1_ffn_W2': _L1_ffn_in['W2'], 'L1_ffn_b2': _L1_ffn_in['b2']}

def reference(x, ctx_768, mask_BxS2_bk0, mask_BxS2_bf1, L0_xattn_ln_x_g, L0_xattn_ln_x_b, L0_xattn_ln_l_g, L0_xattn_ln_l_b, L0_xattn_qn_g, L0_xattn_kn_g, L0_xattn_Wq, L0_xattn_Wkv, L0_xattn_Wlkv, L0_xattn_Wo, L0_xattn_bo, L0_attn_Wq, L0_attn_bq, L0_attn_Wk, L0_attn_bk, L0_attn_Wv, L0_attn_bv, L0_attn_Wg, L0_attn_bg, L0_attn_Wo, L0_attn_bo, L0_ffn_w1, L0_ffn_conv_w, L0_ffn_conv_b, L0_ffn_w2, L1_xattn_Wq, L1_xattn_Wk, L1_xattn_Wv, L1_xattn_Wo, L1_attn_Wqk, L1_attn_bqk, L1_attn_gamma, L1_attn_beta, L1_attn_Wv, L1_attn_bv, L1_attn_rel_emb, L1_ffn_wg, L1_ffn_W1, L1_ffn_b1, L1_ffn_W2, L1_ffn_b2):
    import jax
    import jax.numpy as jnp

    def _L0_xattn_ref(x, latents, mask, ln_x_g, ln_x_b, ln_l_g, ln_l_b, qn_g, kn_g, Wq, Wkv, Wlkv, Wo, bo):
        import jax, jax.numpy as jnp
        import numpy as np
        DIM_IN, DIM_LAT, DIM_HEAD = (192, 256, 64)
        INNER = max(DIM_LAT, DIM_IN)
        HEADS = INNER // DIM_HEAD
        SCALE = DIM_HEAD ** (-0.5)
        RMS_EPS = 1e-08
        LN_EPS = 1e-05

        def layernorm(x, g, b):
            mu = jnp.mean(x, axis=-1, keepdims=True)
            var = jnp.mean((x - mu) ** 2, axis=-1, keepdims=True)
            return (x - mu) * jax.lax.rsqrt(var + LN_EPS) * g + b

        def rmsnorm(x, gamma):
            norm = jnp.sqrt(jnp.sum(x * x, axis=-1, keepdims=True)) * x.shape[-1] ** (-0.5)
            return x / jnp.maximum(norm, RMS_EPS) * gamma
        b, n, _ = x.shape
        m = latents.shape[1]
        xn = layernorm(x, ln_x_g, ln_x_b)
        ln = layernorm(latents, ln_l_g, ln_l_b)
        q = ln @ Wq.T
        kv = jnp.concatenate([xn @ Wkv.T, ln @ Wlkv.T], axis=1)
        k, v = (kv[..., :INNER], kv[..., INNER:])
        split_heads = lambda t: t.reshape(t.shape[0], t.shape[1], HEADS, DIM_HEAD).transpose(0, 2, 1, 3)
        q, k, v = (split_heads(q), split_heads(k), split_heads(v))
        qn = rmsnorm(q, qn_g) * SCALE
        kn = rmsnorm(k, kn_g)
        attn = jnp.einsum('bhid,bhjd->bhij', qn, kn)
        full_mask = jnp.pad(mask, ((0, 0), (0, m)), constant_values=True)
        attn = jnp.where(full_mask[:, None, None, :], attn, -jnp.finfo(attn.dtype).max)
        attn = jax.nn.softmax(attn, axis=-1)
        out = jnp.einsum('bhij,bhjd->bhid', attn, v)
        out = out.transpose(0, 2, 1, 3).reshape(b, m, INNER)
        return out @ Wo.T + bo

    def _L0_attn_ref(x, Wq, bq, Wk, bk, Wv, bv, Wg, bg, Wo, bo):
        import jax, jax.numpy as jnp
        import numpy as np
        EMBED = 256
        HEADS = 16
        HDIM = EMBED // HEADS
        B, S = (4, 1024)
        b, s, _ = x.shape

        def split_heads(t):
            return t.reshape(b, s, HEADS, HDIM).transpose(0, 2, 1, 3)
        q = split_heads(x @ Wq + bq)
        k = split_heads(x @ Wk + bk)
        v = split_heads(x @ Wv + bv)
        q = jax.nn.elu(q) + 1.0
        k = jax.nn.elu(k) + 1.0
        kv = jnp.einsum('bhsd,bhse->bhde', k, v)
        attn = jnp.einsum('bhsd,bhde->bhse', q, kv)
        attn = attn.transpose(0, 2, 1, 3).reshape(b, s, EMBED)
        gate = jax.nn.sigmoid(x @ Wg + bg)
        out = gate * attn @ Wo + bo
        return out

    def _L0_ffn_ref(x, w1, conv_w, conv_b, w2):
        import jax, jax.numpy as jnp
        import numpy as np
        B, S, D_MODEL, D_HIDDEN = (4, 512, 256, 1024)

        def act_quant(x):
            scale = 127.0 / jnp.clip(jnp.max(jnp.abs(x), axis=-1, keepdims=True), 1e-05)
            return jnp.clip(jnp.round(x * scale), -128, 127) / scale

        def weight_quant(w):
            scale = 1.0 / jnp.clip(jnp.mean(jnp.abs(w)), 1e-05)
            return jnp.clip(jnp.round(w * scale), -1, 1) / scale

        def bit_linear(x, w):
            xq = x + jax.lax.stop_gradient(act_quant(x) - x)
            wq = w + jax.lax.stop_gradient(weight_quant(w) - w)
            return jnp.einsum('bsd,hd->bsh', xq, wq)

        def depthwise_conv1d(x_bcl, w, b):
            y = jax.lax.conv_general_dilated(x_bcl, w, window_strides=(1,), padding=[(1, 1)], dimension_numbers=('NCH', 'OIH', 'NCH'), feature_group_count=x_bcl.shape[1])
            return y + b[None, :, None]
        h = bit_linear(x, w1)
        h = depthwise_conv1d(h.transpose(0, 2, 1), conv_w, conv_b)
        h = h.transpose(0, 2, 1)
        h = jax.nn.silu(h)
        return bit_linear(h, w2)

    def _L1_xattn_ref(x, context, context_mask, Wq, Wk, Wv, Wo):
        import jax, jax.numpy as jnp
        import numpy as np
        DIM = 256
        CTX_DIM = 192
        HEADS = 16
        B, N, _ = x.shape
        M = context.shape[1]
        hd = DIM // HEADS
        scale = hd ** (-0.5)
        q = (x @ Wq).reshape(B, N, HEADS, hd).transpose(0, 2, 1, 3)
        k = (context @ Wk).reshape(B, M, HEADS, hd).transpose(0, 2, 1, 3)
        v = (context @ Wv).reshape(B, M, HEADS, hd).transpose(0, 2, 1, 3)
        scores = jnp.einsum('bhid,bhjd->bhij', q, k) * scale
        max_neg = -jnp.finfo(scores.dtype).max
        scores = jnp.where(context_mask[:, None, None, :], scores, max_neg)
        attn = jax.nn.softmax(scores, axis=-1)
        out = jnp.einsum('bhij,bhjd->bhid', attn, v)
        out = out.transpose(0, 2, 1, 3).reshape(B, N, DIM)
        return out @ Wo

    def _L1_attn_ref(x, Wqk, bqk, gamma, beta, Wv, bv, rel_emb):
        import math
        import jax, jax.numpy as jnp
        import numpy as np
        DIM = 256
        DIM_QK = 128
        DIM_V = 256
        NUM_BUCKETS = 32
        MAX_DISTANCE = 128

        def _rel_pos_bucket_causal(seq_len):
            q = np.arange(seq_len)
            n = np.maximum(q[:, None] - q[None, :], 0)
            max_exact = NUM_BUCKETS // 2
            is_small = n < max_exact
            nf = np.maximum(n, 1).astype(np.float32)
            val_if_large = max_exact + (np.log(nf / max_exact) / math.log(MAX_DISTANCE / max_exact) * (NUM_BUCKETS - max_exact)).astype(np.int32)
            val_if_large = np.minimum(val_if_large, NUM_BUCKETS - 1)
            return jnp.asarray(np.where(is_small, n, val_if_large), dtype=jnp.int32)

        def laplacian_attn_fn(x):
            mu = math.sqrt(0.5)
            std = math.sqrt(0.25 * math.pi)
            return (1.0 + jax.lax.erf((x - mu) / (std * math.sqrt(2.0)))) * 0.5
        B, S, _ = x.shape
        qk = jax.nn.swish(jnp.einsum('bsd,de->bse', x, Wqk) + bqk)
        q = qk * gamma[0] + beta[0]
        k = qk * gamma[1] + beta[1]
        v = jax.nn.swish(jnp.einsum('bsd,de->bse', x, Wv) + bv)
        scale = 1.0 / S
        sim = jnp.einsum('bid,bjd->bij', q, k) * scale
        buckets = _rel_pos_bucket_causal(S)
        bias = rel_emb[buckets, 0] * DIM_QK ** 0.5
        sim = sim + bias
        attn = laplacian_attn_fn(sim)
        i = jnp.arange(S)
        future = i[None, :] > i[:, None]
        attn = jnp.where(future, 0.0, attn)
        return jnp.einsum('bij,bjd->bid', attn, v)

    def _L1_ffn_ref(x, wg, W1, b1, W2, b2):
        import jax, jax.numpy as jnp
        import numpy as np
        CAPACITY_FACTOR = 1.25
        B, T, D = x.shape
        E = wg.shape[1]
        N = B * T
        capacity = int(N / E * CAPACITY_FACTOR) + 1
        xf = x.reshape(N, D)
        logits = xf @ wg
        scores = jax.nn.softmax(logits, axis=-1)
        top1 = jnp.argmax(scores, axis=-1)
        combine_w = jnp.take_along_axis(scores, top1[:, None], axis=1)[:, 0]
        oh = jax.nn.one_hot(top1, E, dtype=jnp.int32)
        rank = jnp.take_along_axis(jnp.cumsum(oh, axis=0), top1[:, None], axis=1)[:, 0] - 1
        valid = rank < capacity
        trash = E * capacity
        slot = jnp.where(valid, top1 * capacity + rank, trash)
        buf = jnp.zeros((E * capacity + 1, D), dtype=x.dtype).at[slot].set(xf)
        eb = buf[:E * capacity].reshape(E, capacity, D)
        h = jax.nn.gelu(jnp.einsum('ecd,edf->ecf', eb, W1) + b1[:, None, :], approximate=False)
        y = jnp.einsum('ecf,efd->ecd', h, W2) + b2[:, None, :]
        yf = y.reshape(E * capacity, D)
        gathered = yf[jnp.minimum(slot, E * capacity - 1)]
        out_flat = jnp.where(valid[:, None], gathered, 0.0) * combine_w[:, None]
        return out_flat.reshape(B, T, D)
    x = x + _L0_xattn_ref(ctx_768, _layernorm(x, axis=-1), mask_BxS2_bk0, L0_xattn_ln_x_g, L0_xattn_ln_x_b, L0_xattn_ln_l_g, L0_xattn_ln_l_b, L0_xattn_qn_g, L0_xattn_kn_g, L0_xattn_Wq, L0_xattn_Wkv, L0_xattn_Wlkv, L0_xattn_Wo, L0_xattn_bo)
    x = x + _L0_attn_ref(_layernorm(x, axis=-1), L0_attn_Wq, L0_attn_bq, L0_attn_Wk, L0_attn_bk, L0_attn_Wv, L0_attn_bv, L0_attn_Wg, L0_attn_bg, L0_attn_Wo, L0_attn_bo)
    x = x + _L0_ffn_ref(_layernorm(x, axis=-1), L0_ffn_w1, L0_ffn_conv_w, L0_ffn_conv_b, L0_ffn_w2)
    x = x + _L1_xattn_ref(_layernorm(x, axis=-1), ctx_768, mask_BxS2_bf1, L1_xattn_Wq, L1_xattn_Wk, L1_xattn_Wv, L1_xattn_Wo)
    x = x + _L1_attn_ref(_layernorm(x, axis=-1), L1_attn_Wqk, L1_attn_bqk, L1_attn_gamma, L1_attn_beta, L1_attn_Wv, L1_attn_bv, L1_attn_rel_emb)
    x = x + _L1_ffn_ref(_layernorm(x, axis=-1), L1_ffn_wg, L1_ffn_W1, L1_ffn_b1, L1_ffn_W2, L1_ffn_b2)
    return x

_drawn_inputs = setup_inputs


def setup_inputs(seed=0):
    import zlib

    import numpy as np

    out = dict(_drawn_inputs(seed))
    spreads = {'L0_xattn_ln_x_g': (1.0, 0.2),
     'L0_xattn_ln_x_b': (0.0, 0.1),
     'L0_xattn_ln_l_g': (1.0, 0.2),
     'L0_xattn_ln_l_b': (0.0, 0.1),
     'L0_xattn_qn_g': (1.0, 0.6),
     'L0_xattn_kn_g': (1.0, 0.6),
     'L0_xattn_bo': (0.0, 0.1),
     'L1_attn_bqk': (0.0, 2.0),
     'L1_attn_beta': (0.0, 2.0),
     'L1_attn_bv': (0.0, 0.8),
     'L1_ffn_b1': (0.0, 2.0),
     'L1_ffn_b2': (0.0, 2.0)}
    factors = {'L0_attn_bq': 8.0,
     'L0_attn_bk': 8.0,
     'L0_attn_bg': 3.554,
     'L0_attn_bo': 8.0,
     'L0_ffn_w1': 8.0,
     'L0_ffn_conv_w': 8.0,
     'L0_ffn_conv_b': 8.0,
     'L0_ffn_w2': 8.0,
     'L1_xattn_Wq': 8.0,
     'L1_xattn_Wk': 8.0,
     'L1_xattn_Wv': 7.911,
     'L1_xattn_Wo': 7.91,
     'L1_attn_Wqk': 39.357,
     'L1_attn_gamma': 39.429,
     'L1_attn_rel_emb': 23.314,
     'L1_ffn_wg': 8.0,
     'L1_ffn_W1': 8.0,
     'L1_ffn_W2': 8.0}
    for name, (base, spread) in spreads.items():
        noise = np.random.default_rng([zlib.crc32(name.encode()), seed]).standard_normal(out[name].shape)
        drawn = base * np.exp(spread * noise) if base else spread * noise
        out[name] = jnp.asarray(drawn.astype(out[name].dtype))
    for name, factor in factors.items():
        out[name] = (out[name] * factor).astype(out[name].dtype)
    return out
```

```python
import numpy as np

import concourse.bass as bass
from concourse import mybir
from contextlib import ExitStack
from itertools import zip_longest

F32 = mybir.dt.float32
F32R = mybir.dt.float32r
BF16 = mybir.dt.bfloat16
U8 = mybir.dt.uint8
U32 = mybir.dt.uint32
I32 = mybir.dt.int32
ALU = mybir.AluOpType
ACT = mybir.ActivationFunctionType
AX = mybir.AxisListType

LN_EPS = 1e-5
MASKED = -1e30
ROUND = 1.5 * 2.0 ** 23
TOK = 128
GROUP = 2

ROWS = 107


def nth(batch, per_batch, k):
    return batch * per_batch + (k + 1)


class Chain:

    def __init__(self, engine, sem):
        self.engine, self.sem, self.before, self.base, self.k = engine, sem, 0, 0, 0

    def step(self, instruction):
        self.k += 1
        instruction.then_inc(self.sem, 1)
        self.engine.wait_ge(self.sem, self.base + self.k)

    def enter(self, i, per_round):
        self.before += self.k
        self.base, self.k = i * per_round + self.before, 0

    def leave(self, rounds, per_round):
        assert self.k == per_round, (self.k, per_round)
        self.before += rounds * per_round
        self.base, self.k = self.before, 0


def wait_apart(engine):
    engine.nop(nofuse=True)


def newton_rsqrt(chain, dve, y, v, t):
    chain.step(dve.tensor_tensor(t, y, y, ALU.mult))
    chain.step(dve.tensor_tensor(t, t, v, ALU.mult))
    chain.step(dve.tensor_scalar(t, t, -0.5, 1.5, ALU.mult, ALU.add))
    chain.step(dve.tensor_tensor(y, y, t, ALU.mult))


class Memory:

    def __init__(self, nc, ctx, stage):
        self.nc, self.ctx, self.stage, self.sems = nc, ctx, stage, {}
        ctx.callback(self.release)

    def sbuf(self, name, shape, dtype=F32):
        return self.ctx.enter_context(self.nc.sbuf_tensor(f"{self.stage}_{name}", shape, dtype))

    def psum(self, name, shape, dtype=F32):
        return self.ctx.enter_context(self.nc.psum_tensor(f"{self.stage}_{name}", shape, dtype))

    def sem(self, name):
        if name not in self.sems:
            self.sems[name] = self.nc.alloc_semaphore(f"{self.stage}_{name}")
        return self.sems[name]

    def release(self):
        self.nc.clear_and_free_semaphores(list(self.sems.values()))
        self.nc.all_engine_barrier()


EXP_AND_LN = 6


def load_exp_and_ln(nc):
    nc.scalar.add_instruction(mybir.InstLoadActFuncSet(
        name=nc.get_next_instruction_name(), engine=mybir.EngineType.Activation, act_func_set_id=EXP_AND_LN, ins=[], outs=[]))


class Stream:

    def __init__(self, m, number):
        self.m, self.number = m, number

    def sbuf(self, name, shape, dtype=F32):
        return self.m.sbuf(f"{name}{self.number}", shape, dtype)

    def psum(self, name, shape, dtype=F32):
        return self.m.psum(f"{name}{self.number}", shape, dtype)

    def sem(self, name):
        return self.m.sem(f"{name}{self.number}")


def in_turn(work, streams, r, *more):
    for _ in zip_longest(*(work(b, r, *more) for b in streams)):
        pass




class NormBuffers:

    def __init__(self, m):
        self.stats = m.sbuf("ln_stats", [TOK, GROUP, 6])
        self.moments = m.sbuf("ln_moments", [TOK, GROUP, 2])
        self.var = m.sbuf("ln_var", [TOK, GROUP])
        self.rstd = m.sbuf("ln_rstd", [TOK, GROUP])
        self.tmp = m.sbuf("ln_tmp", [TOK, GROUP])


def layer_norm_vector(nc, chain, sem, tag, nb, X, Y, r):
    v = nc.vector
    for t in range(GROUP):
        i = v.bn_stats(nb.stats[:, t, :], X[:, t, :])
    chain.step(i)
    wait_apart(chain.engine)
    for t in range(GROUP):
        i = v.bn_aggr(nb.moments[:, t, :], nb.stats[:, t, :])
    chain.step(i)
    v.tensor_scalar(nb.var[:], nb.moments[:, :, 1], LN_EPS, None, ALU.add).then_inc(sem(tag + "_var"), 1)
    yield
    chain.engine.wait_ge(sem(tag + "_rstd"), r + 1)
    newton_rsqrt(chain, v, nb.rstd[:], nb.var[:], nb.tmp[:])
    for t in range(GROUP):
        i = v.tensor_scalar(Y[:, t, :], X[:, t, :], nb.moments[:, t, 0:1], nb.rstd[:, t:t + 1], ALU.subtract, ALU.mult)
    i.then_inc(sem(tag + "_norm"), 1)
    chain.engine.wait_ge(sem(tag + "_norm"), r + 1)


def layer_norm_scalar(nc, act, sem, tag, nb, r):
    yield
    act.wait_ge(sem(tag + "_var"), r + 1)
    nc.scalar.activation(nb.rstd[:], nb.var[:], ACT.Ln).then_inc(sem(tag + "_ln"), 1)
    yield
    act.wait_ge(sem(tag + "_ln"), r + 1)
    nc.scalar.activation(nb.rstd[:], nb.rstd[:], ACT.Exp, scale=-0.5).then_inc(sem(tag + "_rstd"), 1)


def transpose_group(nc, out, X, ident):
    for k in range(2):
        for t in range(GROUP):
            i = nc.tensor.transpose(out[:, k, TOK * t:TOK * t + TOK], X[:, t, 128 * k:128 * k + 128], ident[:])
    return i


def by_token(nc, out, xT, w, halves=2):
    for t in range(GROUP):
        for k in range(halves):
            i = nc.tensor.matmul(out[:, t, :], xT[:, k, TOK * t:TOK * t + TOK], w[:, k, :], start=k == 0, stop=k == halves - 1)
    return i


def by_dim(nc, out, xT, w, halves=2):
    for o in range(out.shape[1]):
        for k in range(halves):
            i = nc.tensor.matmul(out[:, o, :], w[:, k, 128 * o:128 * o + 128], xT[:, k, :], start=k == 0, stop=k == halves - 1)
    return i


def tiles_of(x, r):
    return x[bass.ds(r * (GROUP * TOK), GROUP * TOK), :].rearrange("(t p) n -> p t n", p=TOK)


def halves_of(xT, r):
    return xT[:, bass.ds(r * (GROUP * TOK), GROUP * TOK)].rearrange("(k p) n -> p k n", p=128)


def latent_projections(nc, consts, x, ln_g, ln_b, qn_g, kn_g, WqT, WlkvT, qT, klT, vl):
    N, D = x.shape
    GT = GROUP * TOK
    with ExitStack() as ctx:
        m = Memory(nc, ctx, "lp")
        sem = m.sem
        ident = m.sbuf("ident", [128, 128])
        wq = m.sbuf("wq", [128, 2, 256])
        wl = m.sbuf("wl", [128, 2, 512])
        gn = m.sbuf("gn", [128, 256])
        bn = m.sbuf("bn", [128, 256])
        qg = m.sbuf("qg", [128, 64])
        kg = m.sbuf("kg", [128, 64])
        gain = m.sbuf("gain", [128, 64])
        streams = [Stream(m, k) for k in range(2)]
        for b in streams:
            b.xs = b.sbuf("xs", [TOK, GROUP, 256])
            b.l1 = b.sbuf("l1", [TOK, GROUP, 256])
            b.l2 = b.sbuf("l2", [TOK, GROUP, 256])
            b.lT = b.sbuf("lT", [128, 2, GT])
            b.sq = b.sbuf("sq", [TOK, 2 * GROUP, 256])
            b.qk = b.sbuf("qk", [TOK, 2 * GROUP, 256])
            b.ms = b.sbuf("ms", [TOK, 2 * GROUP * 4])
            b.rn = b.sbuf("rn", [TOK, 2 * GROUP * 4])
            b.rt = b.sbuf("rt", [TOK, 2 * GROUP * 4])
            b.qkT = b.sbuf("qkT", [128, 2, 2, GT])
            b.vs = b.sbuf("vs", [TOK, GROUP, 256])
            b.nb = NormBuffers(b)
            b.pT = b.psum("pT", [128, 2, GT])
            b.pV = b.psum("pV", [TOK, GROUP, 256])
            b.pQK = b.psum("pQK", [TOK, 2 * GROUP, 256])
        R = N // (2 * GT)

        block = ctx.enter_context(nc.Block())

        @block.sync
        def _(sp):
            for dst, src in ((ident[:], consts["ident"]), (wq[:], WqT.rearrange("(k p) n -> p k n", p=128)),
                             (wl[:], WlkvT.rearrange("(k p) n -> p k n", p=128)), (gn[:], ln_g.partition_broadcast(128)),
                             (bn[:], ln_b.partition_broadcast(128)), (qg[:], qn_g.partition_broadcast(128)),
                             (kg[:], kn_g.partition_broadcast(128))):
                sp.dma_start(dst, src).then_inc(sem("const_in"), 16)
            def load(b, r):
                sp.dma_start(b.xs[:], tiles_of(x, 2 * r + b.number)).then_inc(b.sem("x_in"), 16)

            def work(b, r, more):
                if more:
                    sp.wait_ge(b.sem("b_var"), r + 1)
                    wait_apart(sp)
                    load(b, r + 1)
                yield
                sp.wait_ge(b.sem("qT"), r + 1)
                wait_apart(sp)
                sp.dma_start(halves_of(qT, 2 * r + b.number), b.qkT[:, 0]).then_inc(b.sem("q_out"), 16)
                yield
                sp.wait_ge(b.sem("kT"), r + 1)
                wait_apart(sp)
                sp.dma_start(halves_of(klT, 2 * r + b.number), b.qkT[:, 1]).then_inc(b.sem("q_out"), 16)
                yield
                sp.wait_ge(b.sem("vs"), r + 1)
                wait_apart(sp)
                sp.dma_start(tiles_of(vl, 2 * r + b.number), b.vs[:]).then_inc(b.sem("q_out"), 16)
            for b in streams:
                load(b, 0)

            with sp.Fori(0, R - 1) as r:
                in_turn(work, streams, r, True)
            in_turn(work, streams, R - 1, False)
            for b in streams:
                sp.wait_ge(b.sem("q_out"), 48 * R)

        @block.scalar
        def _(act):
            load_exp_and_ln(nc)
            act.wait_ge(sem("const_in"), 112)
            def work(b, r):
                yield from layer_norm_scalar(nc, act, b.sem, "a", b.nb, r)
                yield from layer_norm_scalar(nc, act, b.sem, "b", b.nb, r)
                yield
                act.wait_ge(b.sem("lT_ps"), r + 1)
                nc.scalar.activation(b.lT[:], b.pT[:], ACT.Copy).then_inc(b.sem("lT"), 1)
                yield
                act.wait_ge(b.sem("qk_ps"), r + 1)
                nc.scalar.activation(b.sq[:], b.pQK[:], ACT.Square).then_inc(b.sem("sq"), 1)
                yield
                act.wait_ge(b.sem("v_ps"), r + 1)
                act.wait_ge(b.sem("q_out"), 48 * r)
                nc.scalar.activation(b.vs[:], b.pV[:], ACT.Copy).then_inc(b.sem("vs"), 1)
                yield
                act.wait_ge(b.sem("ms"), r + 1)
                nc.scalar.activation(b.rn[:], b.ms[:], ACT.Ln).then_inc(b.sem("rln"), 1)
                yield
                act.wait_ge(b.sem("rln"), r + 1)
                nc.scalar.activation(b.rn[:], b.rn[:], ACT.Exp, scale=-0.5).then_inc(b.sem("rn"), 1)
                yield
                act.wait_ge(b.sem("qT_ps"), r + 1)
                nc.scalar.activation(b.qkT[:, 0], b.pT[:], ACT.Copy).then_inc(b.sem("qT"), 1)

            with act.Fori(0, R) as r:
                in_turn(work, streams, r)
        @block.tensor
        def _(pe):
            pe.wait_ge(sem("const_in"), 112)
            def work(b, r):
                pe.wait_ge(b.sem("l2"), r + 1)
                pe.wait_ge(b.sem("qT"), r)
                transpose_group(nc, b.pT, b.l2, ident).then_inc(b.sem("lT_ps"), 1)
                yield
                pe.wait_ge(b.sem("lT"), r + 1)
                pe.wait_ge(b.sem("qk"), r)
                by_token(nc, b.pQK[:, 0:GROUP], b.lT, wq)
                by_token(nc, b.pQK[:, GROUP:2 * GROUP], b.lT, wl[:, :, 0:256]).then_inc(b.sem("qk_ps"), 1)
                yield
                pe.wait_ge(b.sem("kT"), r)
                by_token(nc, b.pV, b.lT, wl[:, :, 256:512]).then_inc(b.sem("v_ps"), 1)
                yield
                pe.wait_ge(b.sem("qk"), r + 1)
                transpose_group(nc, b.pT, b.qk[:, 0:GROUP], ident).then_inc(b.sem("qT_ps"), 1)
                yield
                pe.wait_ge(b.sem("vs"), r + 1)
                transpose_group(nc, b.pV[:].rearrange("p t n -> p (t n)").rearrange("p (k n) -> p k n", k=2), b.qk[:, GROUP:2 * GROUP], ident).then_inc(b.sem("kT_ps"), 1)

            with pe.Fori(0, R) as r:
                in_turn(work, streams, r)
        @block.vector
        def _(dve):
            v = nc.vector
            chain = Chain(dve, sem("dve"))
            dve.wait_ge(sem("const_in"), 112)
            chain.step(v.tensor_tensor(gain[:], qg[:], kg[:], ALU.mult))
            chain.step(v.tensor_scalar(gain[:], gain[:], 0.125, None, ALU.mult))
            PER = 19
            for b in streams:
                b.chain = Chain(dve, b.sem("dve"))
            def work(b, r):
                dve.wait_ge(b.sem("x_in"), 16 * (r + 1))
                yield from layer_norm_vector(nc, b.chain, b.sem, "a", b.nb, b.xs, b.l1, r)
                yield
                dve.wait_ge(b.sem("lT_ps"), r)
                yield from layer_norm_vector(nc, b.chain, b.sem, "b", b.nb, b.l1, b.l2, r)
                b.chain.step(v.tensor_tensor(b.l2[:], b.l2[:], gn[:].unsqueeze(1).to_broadcast([TOK, GROUP, 256]), ALU.mult))
                v.tensor_tensor(b.l2[:], b.l2[:], bn[:].unsqueeze(1).to_broadcast([TOK, GROUP, 256]), ALU.add).then_inc(b.sem("l2"), 1)
                yield
                dve.wait_ge(b.sem("sq"), r + 1)
                b.chain.step(v.tensor_reduce(b.ms[:], b.sq[:].rearrange("p t (h d) -> p (t h) d", d=64), AX.X, ALU.add))
                v.tensor_scalar(b.ms[:], b.ms[:], 1.0 / 64, 1e-16, ALU.mult, ALU.max).then_inc(b.sem("ms"), 1)
                yield
                dve.wait_ge(b.sem("rn"), r + 1)
                newton_rsqrt(b.chain, v, b.rn[:], b.ms[:], b.rt[:])
                yield
                dve.wait_ge(b.sem("kT_ps"), r)
                heads = b.qk[:].rearrange("p t (h d) -> p (t h) d", d=64)
                b.chain.step(v.tensor_tensor(heads, b.pQK[:].rearrange("p t (h d) -> p (t h) d", d=64),
                                           b.rn[:].unsqueeze(2).to_broadcast([TOK, 8 * GROUP, 64]), ALU.mult))
                v.tensor_tensor(heads[:, 0:4 * GROUP], heads[:, 0:4 * GROUP], gain[:].unsqueeze(1).to_broadcast([TOK, 4 * GROUP, 64]), ALU.mult).then_inc(b.sem("qk"), 1)
                yield
                dve.wait_ge(b.sem("kT_ps"), r + 1)
                dve.wait_ge(b.sem("q_out"), 48 * r)
                v.tensor_copy(b.qkT[:, 1], b.pV[:].rearrange("p t n -> p (t n)").rearrange("p (k n) -> p k n", k=2)).then_inc(b.sem("kT"), 1)

            with dve.Fori(0, R) as r:
                for b in streams:
                    b.chain.enter(r, PER)
                in_turn(work, streams, r)
            for b in streams:
                b.chain.leave(R, PER)



KEYS = 124
CHUNKS = [(0, 4), (4, 3), (7, 3), (10, 3)]
NKT = 13


def latent_cross_attention(nc, consts, ctx_x, mask, g, b, WkvT, qT, klT, vl, oT):
    NB, S2, DC = ctx_x.shape
    H = DC // 2
    PAD = NKT * KEYS
    LAST = S2 - (NKT - 1) * KEYS
    L = qT.shape[1] // NB
    NS = 7
    with ExitStack() as ctx:
        m = Memory(nc, ctx, "xa")
        sem = m.sem
        ident = m.sbuf("ident", [128, 128])
        raw = m.sbuf("raw", [128, NKT, DC])
        xhat = m.sbuf("xhat", [128, 2, NKT, DC + 1])
        stats = m.sbuf("stats", [128, NKT, 6])
        moments = m.sbuf("moments", [128, NKT, 2])
        var = m.sbuf("var", [128, NKT])
        rstd = m.sbuf("rstd", [128, NKT])
        rtmp = m.sbuf("rtmp", [128, NKT])
        xT = m.sbuf("xT", [H + 1, 2, 2, 4 * KEYS])
        w_raw = m.sbuf("w_raw", [H, 2, 512])
        gcol = m.sbuf("gcol", [H, 2])
        bcol = m.sbuf("bcol", [H, 2])
        bwide = m.sbuf("bwide", [H, 2, H + 1])
        wf = m.sbuf("wf", [H + 1, 2, 512])
        ksb = m.sbuf("ksb", [128, 2, 4, 256])
        ksq = m.sbuf("ksq", [128, 4, 256])
        kss = m.sbuf("kss", [128, 2, 16])
        krn = m.sbuf("krn", [128, 2, 16])
        ktmp = m.sbuf("ktmp", [128, 16])
        khat = m.sbuf("khat", [128, 4, 256])
        kT = m.sbuf("kT", [128, 2, 2, PAD + L])
        kTr = m.sbuf("kTr", [128, 2, 4 * KEYS], F32R)
        klTr = m.sbuf("klTr", [128, 2, 2, L], F32R)
        qblk = m.sbuf("qblk", [128, 2, 2, 128])
        qblkr = m.sbuf("qblkr", [128, 2, 2, 128], F32R)
        vlat = m.sbuf("vlat", [L, 2, 2, 129])
        mask8 = m.sbuf("mask8", [128, 2, PAD], U8)
        mbias = m.sbuf("mbias", [128, 2, PAD], BF16)
        augk = m.sbuf("augk", [96, 2, PAD + L], BF16)
        augq = m.sbuf("augq", [96, 256], BF16)
        maxes = m.sbuf("maxes", [128, 2, 2, 5])
        negmax = m.sbuf("negmax", [128, 2, 33])
        junk = m.sbuf("junk", [128, 2, 4 * KEYS], BF16)
        P = m.sbuf("P", [128, 2, 512])
        rden = m.sbuf("rden", [128, 2])
        accn = m.sbuf("accn", [128, 2, DC + 1])
        latn = m.sbuf("latn", [128, 2, 128])
        accT = m.sbuf("accT", [H + 1, 2, 2, 128])
        o_sb = m.sbuf("o_sb", [128, 2, 2, 128])
        ring = [m.psum(f"ring{k}", [128, 512]) for k in range(4)]
        sc = [m.psum(f"sc{k}", [128, 512]) for k in range(2)]
        acc = m.psum("acc", [128, 2, DC + 1])
        latents = m.psum("latents", [128, 512])
        acc2 = latents[:, 0:258].rearrange("p (o n) -> p o n", o=2)
        scl = latents[:, 384:512]

        ROUNDS = [("T", 0), ("X1", 1), ("M", 0), ("K", 0), ("B", 0), ("X2", 1), ("X1", 2), ("R1", 0), ("T", 1),
                  ("R2", 0), ("B", 1), ("K", 1), ("KT", 0), ("X2", 2), ("B", 2), ("X1", 3), ("R1", 1), ("A", 0),
                  ("T", 2), ("R2", 1), ("B", 3), ("X2", 3), ("K", 2), ("KT", 1), ("X1n", 0), ("R1", 2), ("B", 4),
                  ("A", 1), ("T", 3), ("R2", 2), ("B", 5), ("K", 3), ("X2n", 0), ("R1", 3), ("B", 6), ("KT", 2),
                  ("PVend", 0), ("R2", 3), ("A", 2), ("KT", 3), ("F0", 0), ("F1", 0), ("A", 3), ("AL", 0),
                  ("mred", 0), ("F2", 0)]
        OF_B = ("M", "B", "PVend", "F0", "F1", "F2")
        FILLS = []
        for kind, c in ROUNDS:
            if kind == "T":
                FILLS += [((kind, c, 0), "xT0", 4, c), ((kind, c, 1), "xT1", 4, c)]
            elif kind == "K":
                FILLS += [((kind, c, h), "k_out", 8, 2 * c + h) for h in range(2)]
            elif kind == "KT":
                FILLS += [((kind, c, h), "kT_out", 8, 2 * c + h) for h in range(2)]
            elif kind == "A":
                FILLS += [((kind, c, h), "maxed", 9, 2 * c + h) for h in range(2)]
        assert len(FILLS) % len(ring) == 0
        PLACE = {f[0]: n for n, f in enumerate(FILLS)}

        def schedule(engine_step, loop_engine, chain=None, per_round=0):
            def one(n, p, do_a, do_b, do_next):
                for kind, c in ROUNDS:
                    if kind in OF_B:
                        if do_b:
                            engine_step(kind, c, n, p)
                    elif kind in ("X1n", "X2n"):
                        if do_next:
                            engine_step(kind[:2], c, n + 2, p)
                    elif do_a:
                        engine_step(kind, c, n + 1, 1 - p)
            for kind in ("X1", "X2"):
                engine_step(kind, 0, 0, 0)
            one(-1, 1, True, False, True)
            with loop_engine.Fori(0, (NB - 2) // 2) as i:
                if chain:
                    chain.enter(i, per_round)
                one(i * 2, 0, True, True, True)
                one(i * 2 + 1, 1, True, True, True)
            if chain:
                chain.leave((NB - 2) // 2, per_round)
            one(NB - 2, 0, True, True, False)
            one(NB - 1, 1, False, True, False)

        block = ctx.enter_context(nc.Block())

        @block.sync
        def _(sp):
            sp.dma_start(ident[:], consts["ident"]).then_inc(sem("const_in"), 16)
            sp.dma_start(w_raw[:], WkvT.rearrange("(h p) n -> p h n", p=H)).then_inc(sem("const_in"), 16)
            sp.dma_start(gcol[:], g).then_inc(sem("const_in"), 16)
            sp.dma_start(bcol[:], b).then_inc(sem("const_in"), 16)

            def load_ctx(c, n):
                t0, nt = CHUNKS[c % 4]
                full = nt - (c == 3)
                sp.dma_start(raw[0:KEYS, t0:t0 + full, :],
                             ctx_x[bass.ds(n, 1), t0 * KEYS:(t0 + full) * KEYS, :]
                             .rearrange("o (t p) d -> p (o t) d", p=KEYS)).then_inc(sem(f"raw_in{c}"), 16)
                if c == 3:
                    sp.dma_start(raw[0:LAST, NKT - 1, :],
                                 ctx_x[bass.ds(n, 1), (NKT - 1) * KEYS:S2, :]
                                 .rearrange("o p d -> p (o d)")).then_inc(sem(f"raw_in{c}"), 16)

            def load_small(n, p):
                s = sem(f"small_in{p}")
                sp.dma_start(mask8[:, p, 0:S2], mask[bass.ds(n, 1), :].rearrange("o k -> (o k)").partition_broadcast(128)).then_inc(s, 16)
                cols = bass.ds(n * L, L)
                for h in range(2):
                    src = qT[:, cols].rearrange("(o h p) i -> h p o i", h=2, p=64)
                    sp.dma_start(qblk[64 * h:64 * h + 64, p, :, 64 * h:64 * h + 64], src[h]).then_inc(s, 16)
                sp.dma_start(kT[:, p, :, PAD:PAD + L], klT[:, cols].rearrange("(o p) i -> p o i", p=128)).then_inc(s, 16)
                sp.dma_start(vlat[:, p, :, 0:128], vl[cols, :].rearrange("j (o d) -> j o d", o=2)).then_inc(s, 16)

            sp.wait_ge(sem("zeroed"), 1)
            for c in range(4):
                load_ctx(c, 0)
            load_small(0, 0)
            load_small(1, 1)

            def step(kind, c, n, p):
                if kind == "T":
                    sp.wait_ge(sem("xhat"), nth(n, 4, c))
                    load_ctx(c, n + 1)
                if kind == "F1" and not (isinstance(n, int) and n + 2 >= NB):
                    sp.wait_ge(sem("pv"), nth(n, 7, 6))
                    wait_apart(sp)
                    load_small(n + 2, p)
                if kind == "F2":
                    sp.wait_ge(sem("o_sb"), nth(n, 1, 0))
                    for h in range(2):
                        dst = oT[:, bass.ds(n * L, L)].rearrange("(o h p) i -> h p o i", h=2, p=64)
                        sp.dma_start(dst[h], o_sb[64 * h:64 * h + 64, p, :, 64 * h:64 * h + 64]).then_inc(sem(f"o_out{p}"), 16)
            def limited(kind, c, n, p):
                if isinstance(n, int) and n + 1 >= NB and kind == "T":
                    return
                step(kind, c, n, p)
            schedule(limited, sp)
            sp.wait_ge(sem("o_out0"), 16 * NB)
            sp.wait_ge(sem("o_out1"), 16 * NB)

        @block.gpsimd
        def _(pool):
            nc.gpsimd.memset(raw[:], 0.0)
            nc.gpsimd.memset(mask8[:], 0)
            nc.gpsimd.memset(qblk[:], 0.0)
            nc.gpsimd.memset(vlat[:], 1.0).then_inc(sem("zeroed"), 1)
            nc.gpsimd.memset(xhat[:], 1.0)
            nc.gpsimd.memset(augk[:], 0.0)
            nc.gpsimd.memset(augq[:], 0.0)
            nc.gpsimd.memset(negmax[:], 0.0)
            nc.gpsimd.memset(bwide[:], 0.0).then_inc(sem("set"), 1)
            pool.wait_ge(sem("set"), 1)
            nc.gpsimd.memset(augk[0:1, :, :], 1.0)
            nc.gpsimd.memset(augk[32:33, :, :], 1.0)
            nc.gpsimd.memset(augq[64:65, :], 1.0).then_inc(sem("set"), 1)
            pool.wait_ge(sem("set"), 2)

            def step(kind, c, n, p):
                if kind == "T" and c == 0:
                    pool.wait_ge(sem(f"small_in{p}"), 40 * (n - p) + 80)
                    if not (isinstance(n, int) and n < 2):
                        pool.wait_ge(sem("pv"), (n - 1) * 7)
                    wait_apart(pool)
                    nc.gpsimd.tensor_scalar(mbias[:, p, :], mask8[:, p, :], -1.0, -MASKED, ALU.add, ALU.mult).then_inc(sem("mbias"), 1)
                    nc.gpsimd.tensor_copy(qblkr[:, p], qblk[:, p])
                    nc.gpsimd.tensor_copy(klTr[:, p], kT[:, p, :, PAD:PAD + L]).then_inc(sem("q_r"), 1)
            schedule(step, pool)

        @block.scalar
        def _(act):
            load_exp_and_ln(nc)
            def step(kind, c, n, p):
                t0, nt = CHUNKS[c % 4]
                W = nt * KEYS
                if kind == "X1":
                    act.wait_ge(sem("var"), nth(n, 4, c))
                    nc.scalar.activation(rstd[0:KEYS, t0:t0 + nt], var[0:KEYS, t0:t0 + nt], ACT.Ln).then_inc(sem("ln"), 1)
                    act.wait_ge(sem("ln"), nth(n, 4, c))
                    nc.scalar.activation(rstd[0:KEYS, t0:t0 + nt], rstd[0:KEYS, t0:t0 + nt], ACT.Exp, scale=-0.5).then_inc(sem("rstd0"), 1)
                if kind == "T":
                    f = PLACE["T", c, 0]
                    act.wait_ge(sem("xT_ps"), nth(n, 8, 2 * c))
                    if not (isinstance(n, int) and n == 0 and c < 2):
                        act.wait_ge(sem("k_ps"), nth(n, 8, 2 * (c - 2) + 1))
                    nc.scalar.activation(xT[0:H, c % 2, 0, 0:W], ring[f % len(ring)][0:H, 0:W], ACT.Copy).then_inc(sem("xT0"), 1)
                if kind == "K":
                    for h in range(2):
                        f = PLACE["K", c, h]
                        n2 = min(2, nt - 2 * h)
                        act.wait_ge(sem("k_ps"), nth(n, 8, 2 * c + h))
                        if h == 0 and not (isinstance(n, int) and n == 0 and c < 2):
                            act.wait_ge(sem("khat"), nth(n, 4, c - 2))
                        nc.scalar.activation(ksb[0:KEYS, c % 2, 2 * h:2 * h + n2, :],
                                             ring[f % len(ring)][0:KEYS, 0:256 * n2].rearrange("p (t d) -> p t d", d=256), ACT.Copy)
                        if h == 0 and not (isinstance(n, int) and n == 0 and c == 0):
                            act.wait_ge(sem("ksum"), nth(n, 4, c - 1))
                        nc.scalar.activation(ksq[0:KEYS, 2 * h:2 * h + n2, :],
                                             ring[f % len(ring)][0:KEYS, 0:256 * n2].rearrange("p (t d) -> p t d", d=256),
                                             ACT.Square).then_inc(sem("k_out"), 1)
                if kind == "R1":
                    act.wait_ge(sem("kss"), nth(n, 4, c))
                    r = krn[0:KEYS, c % 2, 0:4 * nt]
                    nc.scalar.activation(r, kss[0:KEYS, c % 2, 0:4 * nt], ACT.Ln).then_inc(sem("kln"), 1)
                    act.wait_ge(sem("kln"), nth(n, 4, c))
                    nc.scalar.activation(r, r, ACT.Exp, scale=-0.5).then_inc(sem("krn0"), 1)
                if kind == "KT":
                    for h in range(2):
                        f = PLACE["KT", c, h]
                        act.wait_ge(sem("kT_ps"), nth(n, 8, 2 * c + h))
                        if h == 0 and c == 0 and not (isinstance(n, int) and n < 2):
                            act.wait_ge(sem("pv"), (n - 1) * 7)
                        nc.scalar.activation(kT[:, p, h, t0 * KEYS:t0 * KEYS + W], ring[f % len(ring)][:, 0:W], ACT.Copy)
                        if h == 0 and not (isinstance(n, int) and n == 0 and c == 0):
                            act.wait_ge(sem("a_ps"), nth(n, 9, 2 * c - 1) if c else (n - 1) * 9 + 8)
                        nc.scalar.activation(kTr[:, h, 0:W], ring[f % len(ring)][:, 0:W], ACT.Copy).then_inc(sem("kT_out"), 1)
                if kind == "B":
                    act.wait_ge(sem("s_ps"), nth(n, 7, c))
                    if not (isinstance(n, int) and n == 0 and c < 2):
                        act.wait_ge(sem("pv"), nth(n, 7, max(c - 2, -1)))
                    s = sc[(c + 1) % 2]
                    if c < 6:
                        nc.scalar.activation(P[0:KEYS, c % 2, :], s[0:KEYS, :], ACT.Exp).then_inc(sem("exped"), 1)
                    else:
                        nc.scalar.activation(P[0:KEYS, c % 2, 0:256], s[0:KEYS, 0:256], ACT.Exp)
                        nc.scalar.activation(P[0:L, c % 2, 256:512], s[0:L, 256:512], ACT.Exp).then_inc(sem("exped"), 1)
                if kind == "F1":
                    act.wait_ge(sem("f1_ps"), nth(n, 1, 0))
                    for h in range(2):
                        i = nc.scalar.activation(accT[0:H + h, h], sc[0][0:H + h, 256 * h:256 * h + 256].rearrange("p (o q) -> p o q", o=2), ACT.Copy)
                    i.then_inc(sem("accT"), 1)
                if kind == "F2":
                    act.wait_ge(sem("f2_ps"), nth(n, 1, 0))
                    if not (isinstance(n, int) and n < 2):
                        act.wait_ge(sem(f"o_out{p}"), 16 * n - 16 * p)
                    nc.scalar.activation(o_sb[:, p], sc[1][:, 0:256].rearrange("p (o q) -> p o q", o=2), ACT.Copy).then_inc(sem("o_sb"), 1)

            schedule(step, act)

        @block.tensor
        def _(pe):
            pe.wait_ge(sem("const_in"), 64)
            pe.wait_ge(sem("wide"), 1)
            for h in range(2):
                i = nc.tensor.matmul(sc[0][0:H + 1, :], bwide[:, h, :], w_raw[:, h, :], start=h == 0, stop=h == 1)
            i.then_inc(sem("bias_ps"), 1)
            pe.wait_ge(sem("wf"), 1)

            def room(key, n):
                f = PLACE[key]
                _, name, per, k = FILLS[f - len(ring)]
                if f >= len(ring):
                    pe.wait_ge(sem(name), nth(n, per, k))
                elif not (isinstance(n, int) and n == 0):
                    pe.wait_ge(sem(name), nth(n - 1, per, k))
                return ring[f % len(ring)]

            def weigh(c, n, p):
                pe.wait_ge(sem("exped"), nth(n, 7, c))
                if c == 0 and not (isinstance(n, int) and n == 0):
                    pe.wait_ge(sem("accn"), n)
                for u in range(2):
                    t = 2 * c + u
                    for o in range(2):
                        w = P[0:KEYS, c % 2, 256 * u + 128 * o:256 * u + 128 * o + 128]
                        if t < NKT:
                            i = nc.tensor.matmul(acc[:, o, :], w, xhat[0:KEYS, p, t, :], start=t == 0 and o == 0,
                                                 stop=t == NKT - 1, skip_group_check=True)
                        else:
                            i = nc.tensor.matmul(acc2[:, o, :], w[0:L], vlat[:, p, o, :], start=o == 0, stop=True, skip_group_check=True)
                i.then_inc(sem("pv"), 1)

            def step(kind, c, n, p):
                t0, nt = CHUNKS[c % 4]
                W = nt * KEYS
                if kind == "T":
                    pe.wait_ge(sem("xhat"), nth(n, 4, c))
                    for h in range(2):
                        bank = room((kind, c, h), n)
                        hi = H + h
                        for t in range(nt):
                            i = nc.tensor.transpose(bank[0:hi, t * KEYS:(t + 1) * KEYS],
                                                    xhat[0:KEYS, p, t0 + t, H * h:H * h + hi], ident[0:KEYS, 0:KEYS])
                        i.then_inc(sem("xT_ps"), 1)
                if kind == "K":
                    pe.wait_ge(sem("xT0"), nth(n, 4, c))
                    pe.wait_ge(sem("xT1"), nth(n, 4, c))
                    for h2 in range(2):
                        bank = room((kind, c, h2), n)
                        for t in range(2 * h2, min(nt, 2 * h2 + 2)):
                            for h in range(2):
                                i = nc.tensor.matmul(bank[0:KEYS, 256 * (t % 2):256 * (t % 2) + 256],
                                                     xT[0:H + h, c % 2, h, t * KEYS:(t + 1) * KEYS], wf[0:H + h, h, 0:256],
                                                     start=h == 0, stop=h == 1)
                        i.then_inc(sem("k_ps"), 1)
                if kind == "KT":
                    pe.wait_ge(sem("khat"), nth(n, 4, c))
                    for o in range(2):
                        bank = room((kind, c, o), n)
                        for t in range(nt):
                            i = nc.tensor.transpose(bank[:, t * KEYS:(t + 1) * KEYS], khat[0:KEYS, t, 128 * o:128 * o + 128],
                                                    ident[0:KEYS, 0:KEYS])
                        i.then_inc(sem("kT_ps"), 1)
                if kind == "A":
                    pe.wait_ge(sem("kT_out"), nth(n, 8, 2 * c + 1))
                    pe.wait_ge(sem("q_r"), nth(n, 1, 0))
                    for o in range(2):
                        bank = room((kind, c, o), n)
                        i = nc.tensor.matmul(bank[:, 0:W], qblkr[:, p, o, :], kTr[:, o, 0:W], start=True, stop=True)
                        i.then_inc(sem("a_ps"), 1)
                if kind == "AL":
                    if not (isinstance(n, int) and n == 0):
                        pe.wait_ge(sem("accn"), n)
                    for o in range(2):
                        i = nc.tensor.matmul(scl[:, 64 * o:64 * o + 64], qblkr[:, p, o, :], klTr[:, p, o, :], start=True, stop=True)
                    i.then_inc(sem("a_ps"), 1)
                if kind == "M":
                    pe.wait_ge(sem("negmax"), nth(n, 1, 0))
                    if not (isinstance(n, int) and n == 0):
                        pe.wait_ge(sem("accT"), n)
                    for o in range(2):
                        i = nc.tensor.matmul(sc[0][0:33, 128 * o:128 * o + 128], negmax[:, o, :], ident[:], start=True, stop=True)
                    i.then_inc(sem("m_ps"), 1)
                if kind == "B":
                    s = sc[(c + 1) % 2]
                    if c == 0:
                        pe.wait_ge(sem("augq"), nth(n, 1, 0))
                        pe.wait_ge(sem("augk"), nth(n, 1, 0))
                        if not (isinstance(n, int) and n == 0):
                            pe.wait_ge(sem("o_sb"), n)
                    elif c >= 2:
                        pe.wait_ge(sem("exped"), nth(n, 7, c - 2))
                    for u in range(2):
                        t = 2 * c + u
                        k0, w = (t * KEYS, KEYS) if t < NKT else (PAD, L)
                        nc.tensor.matmul(s[0:w, 256 * u:256 * u + 256], augk[0:65, p, k0:k0 + w], augq[0:65, :], start=True, stop=True)
                        for o in range(2):
                            i = nc.tensor.matmul(s[0:w, 256 * u + 128 * o:256 * u + 128 * o + 128], kT[:, p, o, k0:k0 + w],
                                                 qblk[:, p, o, :], start=False, stop=True, skip_group_check=True)
                    i.then_inc(sem("s_ps"), 1)
                    if c > 0:
                        weigh(c - 1, n, p)
                if kind == "PVend":
                    weigh(6, n, p)
                if kind == "F1":
                    pe.wait_ge(sem("accn"), nth(n, 1, 0))
                    pe.wait_ge(sem("exped"), nth(n, 7, 5))
                    for h in range(2):
                        for o in range(2):
                            col = 256 * h + 128 * o
                            i = nc.tensor.transpose(sc[0][0:H + h, col:col + 128], accn[:, o, H * h:H * h + H + h], ident[:])
                    i.then_inc(sem("f1_ps"), 1)
                if kind == "F2":
                    pe.wait_ge(sem("accT"), nth(n, 1, 0))
                    pe.wait_ge(sem("exped"), nth(n, 7, 6))
                    for o in range(2):
                        out = sc[1][:, 128 * o:128 * o + 128]
                        for h in range(2):
                            nc.tensor.matmul(out, wf[0:H + h, h, 256 + 128 * o:384 + 128 * o], accT[0:H + h, h, o, :], start=h == 0, stop=False)
                        i = nc.tensor.matmul(out, latn[:, o, :], ident[:], start=False, stop=True)
                    i.then_inc(sem("f2_ps"), 1)
            schedule(step, pe)

        @block.vector
        def _(dve):
            v = nc.vector
            chain = Chain(dve, sem("dve"))
            dve.wait_ge(sem("const_in"), 64)
            dve.wait_ge(sem("set"), 2)
            for h in range(2):
                v.tensor_scalar(wf[0:H, h, :], w_raw[:, h, :], gcol[:, h:h + 1], None, ALU.mult)
                i = v.tensor_copy(bwide[:, h, H:H + 1], bcol[:, h:h + 1])
            i.then_inc(sem("wide"), 1)
            dve.wait_ge(sem("bias_ps"), 1)
            v.tensor_copy(wf[H:H + 1, 1, :], sc[0][H:H + 1, :]).then_inc(sem("wf"), 1)

            def step(kind, c, n, p):
                t0, nt = CHUNKS[c % 4]
                W = nt * KEYS
                if kind == "X1":
                    dve.wait_ge(sem(f"raw_in{c}"), (n + 1) * 16 * (1 + (c == 3)))
                    for t in range(t0, t0 + nt):
                        i = v.bn_stats(stats[0:KEYS, t, :], raw[0:KEYS, t, :])
                    chain.step(i)
                    wait_apart(chain.engine)
                    for t in range(t0, t0 + nt):
                        i = v.bn_aggr(moments[0:KEYS, t, :], stats[0:KEYS, t, :])
                    chain.step(i)
                    v.tensor_scalar(var[0:KEYS, t0:t0 + nt], moments[0:KEYS, t0:t0 + nt, 1], LN_EPS, None, ALU.add).then_inc(sem("var"), 1)
                if kind == "X2":
                    dve.wait_ge(sem("rstd0"), nth(n, 4, c))
                    newton_rsqrt(chain, v, rstd[0:KEYS, t0:t0 + nt], var[0:KEYS, t0:t0 + nt], rtmp[0:KEYS, t0:t0 + nt])
                    if not (isinstance(n, int) and n < 2):
                        dve.wait_ge(sem("pv"), (n - 1) * 7 if c else (n - 2) * 7 + (nt + 1) // 2)
                    for t in range(t0, t0 + nt):
                        i = v.tensor_scalar(xhat[0:KEYS, p, t, 0:DC], raw[0:KEYS, t, :], moments[0:KEYS, t, 0:1],
                                            rstd[0:KEYS, t:t + 1], ALU.subtract, ALU.mult)
                    i.then_inc(sem("xhat"), 1)
                if kind == "T":
                    f = PLACE["T", c, 1]
                    dve.wait_ge(sem("xT_ps"), nth(n, 8, 2 * c + 1))
                    if not (isinstance(n, int) and n == 0 and c < 2):
                        dve.wait_ge(sem("k_ps"), nth(n, 8, 2 * (c - 2) + 1))
                    v.tensor_copy(xT[:, c % 2, 1, 0:W], ring[f % len(ring)][0:H + 1, 0:W]).then_inc(sem("xT1"), 1)
                if kind == "R1":
                    dve.wait_ge(sem("k_out"), nth(n, 8, 2 * c + 1))
                    s_ = kss[0:KEYS, c % 2, 0:4 * nt]
                    v.tensor_reduce(s_, ksq[0:KEYS, 0:nt, :].rearrange("p t (h d) -> p (t h) d", d=64), AX.X, ALU.add).then_inc(sem("ksum"), 1)
                    dve.wait_ge(sem("ksum"), nth(n, 4, c))
                    v.tensor_scalar(s_, s_, 1.0 / 64, 1e-16, ALU.mult, ALU.max).then_inc(sem("kss"), 1)
                if kind == "R2":
                    r = krn[0:KEYS, c % 2, 0:4 * nt]
                    dve.wait_ge(sem("krn0"), nth(n, 4, c))
                    newton_rsqrt(chain, v, r, kss[0:KEYS, c % 2, 0:4 * nt], ktmp[0:KEYS, 0:4 * nt])
                    if not (isinstance(n, int) and n == 0 and c == 0):
                        dve.wait_ge(sem("kT_ps"), nth(n, 8, 2 * c - 1))
                    v.tensor_tensor(khat[0:KEYS, 0:nt, :].rearrange("p t (h d) -> p (t h) d", d=64),
                                    ksb[0:KEYS, c % 2, 0:nt, :].rearrange("p t (h d) -> p (t h) d", d=64),
                                    r.unsqueeze(2).to_broadcast([KEYS, 4 * nt, 64]), ALU.mult).then_inc(sem("khat"), 1)
                if kind == "A":
                    if c == 0:
                        dve.wait_ge(sem("mbias"), nth(n, 1, 0))
                        v.tensor_copy(augk[64:65, p, 0:PAD], mbias[64:65, p, :]).then_inc(sem("augk"), 1)
                    for o in range(2):
                        f = PLACE["A", c, o]
                        dve.wait_ge(sem("a_ps"), nth(n, 9, 2 * c + o))
                        if not (isinstance(n, int) and n == 0 and c == 0):
                            dve.wait_ge(sem("maxed"), nth(n, 9, 2 * (c - 1) + o) if c else nth(n - 1, 9, 6 + o))
                        wait_apart(chain.engine)
                        v.tensor_tensor_reduce(out=junk[:, o, 0:W], in0=ring[f % len(ring)][:, 0:W], in1=mbias[:, p, t0 * KEYS:t0 * KEYS + W],
                                               scale=1.0, scalar=-3.0e38, op0=ALU.add, op1=ALU.max,
                                               accum_out=maxes[:, p, o, c:c + 1]).then_inc(sem("maxed"), 1)
                if kind == "AL":
                    dve.wait_ge(sem("a_ps"), nth(n, 9, 8))
                    v.tensor_reduce(maxes[:, p, :, 4], scl.rearrange("p (o k) -> p o k", o=2),
                                    AX.X, ALU.max).then_inc(sem("maxed"), 1)
                if kind == "mred":
                    dve.wait_ge(sem("maxed"), nth(n, 9, 8))
                    if not (isinstance(n, int) and n == 0):
                        dve.wait_ge(sem("m_ps"), n)
                    for col in (0, 32):
                        i = v.tensor_reduce(negmax[:, :, col], maxes[:, p], AX.X, ALU.max)
                    chain.step(i)
                    for col in (0, 32):
                        i = v.tensor_scalar(negmax[:, :, col], negmax[:, :, col], -1.0, None, ALU.mult)
                    i.then_inc(sem("negmax"), 1)
                if kind == "M":
                    dve.wait_ge(sem("m_ps"), nth(n, 1, 0))
                    if not (isinstance(n, int) and n == 0):
                        dve.wait_ge(sem("s_ps"), n * 7)
                    chain.step(v.tensor_copy(augq[0:33, :], sc[0][0:33, 0:256]))
                    v.tensor_tensor(augq[32:33, :], sc[0][32:33, 0:256], augq[32:33, :], ALU.subtract).then_inc(sem("augq"), 1)
                if kind == "F0":
                    dve.wait_ge(sem("pv"), nth(n, 7, 6))
                    if not (isinstance(n, int) and n == 0):
                        dve.wait_ge(sem("f2_ps"), n)
                    chain.step(v.tensor_copy(rden[:], acc[:, :, DC]))
                    chain.step(v.tensor_tensor(rden[:], acc2[:, :, 128], rden[:], ALU.add))
                    chain.step(v.reciprocal(rden[:], rden[:]))
                    for o in range(2):
                        v.tensor_scalar(accn[:, o, :], acc[:, o, :], rden[:, o:o + 1], None, ALU.mult)
                        i = v.tensor_scalar(latn[:, o, :], acc2[:, o, 0:128], rden[:, o:o + 1], None, ALU.mult)
                    i.then_inc(sem("accn"), 1)
            schedule(step, dve, chain, 90)


def quantizing_scales(nc, chain, am, sc_, s_out, w_mean):
    v = nc.vector
    chain.step(v.tensor_scalar(am, am, 1e-5, None, ALU.max))
    chain.step(v.reciprocal(sc_, am))
    v.tensor_scalar(sc_, sc_, 127.0, None, ALU.mult)
    chain.step(v.tensor_scalar(s_out, am, 1.0 / 127, w_mean, ALU.mult, ALU.mult))


def gated_attention_and_ffn(nc, consts, x, oT, W, x2, q3T):
    N, D = x.shape
    GT = GROUP * TOK
    S = 64
    NBG = GT // S
    R = N // (2 * GT)
    NF = W["w1T"].shape[1] // 128
    with ExitStack() as ctx:
        m = Memory(nc, ctx, "gf")
        sem = m.sem
        ident = m.sbuf("ident", [128, 128])
        identb = m.sbuf("identb", [128, 128], BF16)
        ones = m.sbuf("ones", [128, 128])
        hmask = m.sbuf("hmask", [128, 128])
        wm = {k: m.sbuf(k, [128, 2, 256]) for k in ("WoT0", "Wq", "Wk", "Wv", "Wg", "Wo", "Wq3")}
        bias = {k: m.sbuf(k, [128, 256]) for k in ("bo0", "bk", "bv", "bg", "bo")}
        bq = m.sbuf("bq", [128, 2])
        w1 = m.sbuf("w1", [128, 2, 1024])
        w2 = m.sbuf("w2", [128, NF, 256])
        w1q = m.sbuf("w1q", [128, 2, 1024], BF16)
        w2q = m.sbuf("w2q", [128, NF, 256], BF16)
        conv = m.sbuf("conv", [128, NF, 4])
        wsum = m.sbuf("wsum", [128, 2])
        wmean = m.sbuf("wmean", [128, 2])
        wscale = m.sbuf("wscale", [128, 2])
        streams = [Stream(m, k) for k in range(2)]
        for b in streams:
            b.h2 = b.sbuf("h2", [128, NF, GT])
            b.h2r = b.sbuf("h2r", [128, NF, GT])
            b.h2q = b.sbuf("h2q", [128, NF, GT], BF16)
            b.xs = b.sbuf("xs", [TOK, GROUP, 256])
            b.os_ = b.sbuf("os", [128, 2, GT])
            b.x1 = b.sbuf("x1", [TOK, GROUP, 256])
            b.ln = b.sbuf("ln", [TOK, GROUP, 256])
            b.lT = b.sbuf("lT", [128, 2, GT])
            b.qe = b.sbuf("qe", [128, 2, GT])
            b.qp = b.sbuf("qp", [128, 2, GT])
            b.kb = b.sbuf("kb", [TOK, GROUP, 256])
            b.ke = b.sbuf("ke", [TOK, GROUP, 256])
            b.vb = b.sbuf("vb", [TOK, GROUP, 256])
            b.gb = b.sbuf("gb", [TOK, GROUP, 256])
            b.kvm = b.sbuf("kvm", [128, 2 * NBG, 128])
            b.xq = b.sbuf("xq", [TOK, GROUP, 256], BF16)
            b.xqT = b.sbuf("xqT", [128, 2, GT], BF16)
            b.am = b.sbuf("am", [TOK, GROUP])
            b.qs = b.sbuf("qs", [TOK, GROUP])
            b.s1 = b.sbuf("s1", [TOK, GROUP])
            b.am2 = b.sbuf("am2", [TOK, GROUP])
            b.qs2 = b.sbuf("qs2", [TOK, GROUP])
            b.s2 = b.sbuf("s2", [TOK, GROUP])
            b.diag = b.sbuf("diag", [128, GROUP, 128])
            b.srow = b.sbuf("srow", [128, GT])
            b.srow2 = b.sbuf("srow2", [128, GT])
            b.padded = b.sbuf("padded", [128, 3, NBG, S + 2])
            b.cv = b.sbuf("cv", [128, 3, NBG, S])
            b.mx = b.sbuf("mx", [128, GT])
            b.q3 = b.sbuf("q3", [128, 2, GT])
            b.nb = NormBuffers(b)
            b.pA, b.pB, b.pC, b.pD = (b.psum(f"p{k}", [128, 512]) for k in "ABCD")

        def tok(p):
            return p[:].rearrange("p (t n) -> p t n", t=GROUP)

        def dim(p):
            return p[:].rearrange("p (k n) -> p k n", k=2)

        def wide(name):
            return bias[name][:].unsqueeze(1).to_broadcast([TOK, GROUP, 256])

        loads = [(ident[:], consts["ident"]), (hmask[:], consts["head16"]), (bq[:], W["bq"]), (conv[:], W["conv"]),
                 (w1[:], W["w1T"].rearrange("(k p) n -> p k n", p=128)), (w2[:], W["w2T"].rearrange("(k p) n -> p k n", p=128))]
        loads += [(wm[k][:], W[k].rearrange("(k p) n -> p k n", p=128)) for k in wm]
        loads += [(bias[k][:], W[k].partition_broadcast(128)) for k in bias]
        NL = 16 * len(loads)
        def bank(b, f):
            return (b.pB, b.pC, b.pA)[f % 3][:, 0:GT]


        block = ctx.enter_context(nc.Block())

        @block.sync
        def _(sp):
            for dst, src in loads:
                sp.dma_start(dst, src).then_inc(sem("const_in"), 16)
            def load(b, r):
                sp.dma_start(b.xs[:], tiles_of(x, 2 * r + b.number)).then_inc(b.sem("x_in"), 16)
                sp.dma_start(b.os_[:], halves_of(oT, 2 * r + b.number)).then_inc(b.sem("x_in"), 16)

            def work(b, r, more):
                if more:
                    sp.wait_ge(b.sem("a_var"), r + 1)
                    wait_apart(sp)
                    load(b, r + 1)
                yield
                sp.wait_ge(b.sem("x2"), r + 1)
                wait_apart(sp)
                sp.dma_start(tiles_of(x2, 2 * r + b.number), b.x1[:]).then_inc(b.sem("x2_out"), 16)
                yield
                sp.wait_ge(b.sem("q3"), r + 1)
                wait_apart(sp)
                sp.dma_start(halves_of(q3T, 2 * r + b.number), b.q3[:]).then_inc(b.sem("q3_out"), 16)
            for b in streams:
                load(b, 0)

            with sp.Fori(0, R - 1) as r:
                in_turn(work, streams, r, True)
            in_turn(work, streams, R - 1, False)
            for b in streams:
                sp.wait_ge(b.sem("x2_out"), 16 * R)
                sp.wait_ge(b.sem("q3_out"), 16 * R)

        @block.gpsimd
        def _(pool):
            nc.gpsimd.memset(ones[:], 1.0)
            nc.gpsimd.memset(streams[1].padded[:], 0.0)
            nc.gpsimd.memset(streams[0].padded[:], 0.0).then_inc(sem("set"), 1)

        @block.scalar
        def _(act):
            act.wait_ge(sem("const_in"), NL)
            nc.scalar.activation(streams[0].h2r[:], w1[:].rearrange("p k (a n) -> p (k a) n", n=GT), ACT.Abs, accum_out=wsum[:, 0:1])
            nc.scalar.activation(streams[1].h2r[:], w2[:], ACT.Abs, accum_out=wsum[:, 1:2]).then_inc(sem("wsum"), 1)
            nc.scalar.activation(identb[:], ident[:], ACT.Copy).then_inc(sem("identb"), 1)
            act.wait_ge(sem("set"), 1)
            def work(b, r):
                if b.number == 0:
                    load_exp_and_ln(nc)
                yield from layer_norm_scalar(nc, act, b.sem, "a", b.nb, r)
                yield
                act.wait_ge(b.sem("lT_ps"), 4 * r + 1)
                nc.scalar.activation(b.lT[:], dim(b.pB), ACT.Copy).then_inc(b.sem("lT"), 1)
                yield
                act.wait_ge(b.sem("qb"), r + 1)
                nc.scalar.activation(b.qe[:], b.qp[:], ACT.Exp).then_inc(b.sem("qe"), 1)
                yield
                act.wait_ge(b.sem("kb"), r + 1)
                nc.scalar.activation(b.ke[:], b.kb[:], ACT.Exp).then_inc(b.sem("ke"), 1)
                yield
                act.wait_ge(b.sem("gb"), r + 1)
                nc.scalar.activation(b.gb[:], b.gb[:], ACT.Sigmoid).then_inc(b.sem("gs"), 1)
                yield
                act.wait_ge(b.sem("lT_ps"), 4 * r + 2)
                nc.scalar.activation(b.lT[:], dim(b.pB), ACT.Copy).then_inc(b.sem("lT"), 1)
                if b.number == 0:
                    load_exp_and_ln(nc)
                yield from layer_norm_scalar(nc, act, b.sem, "b", b.nb, r)
                yield
                act.wait_ge(b.sem("s_ps"), 2 * r + 1)
                nc.scalar.activation(b.srow[:], b.pD[:, 0:GT], ACT.Copy).then_inc(b.sem("srow"), 1)
                yield
                act.wait_ge(b.sem("lT_ps"), 4 * r + 3)
                nc.scalar.activation(b.xqT[:], b.pA[:, 0:GT].bitcast(BF16).rearrange("p (k n) -> p k n", k=2), ACT.Copy).then_inc(b.sem("xqT"), 1)

                def silu(f):
                    act.wait_ge(b.sem("conv"), r * NF + f + 1)
                    nc.scalar.activation(b.h2[:, f, :], b.cv[:, f % 3].rearrange("p b s -> p (b s)"), ACT.Silu).then_inc(b.sem("h2"), 1)
                for f in range(NF):
                    yield
                    act.wait_ge(b.sem("hs"), r * NF + f + 1)
                    if f >= 3:
                        act.wait_ge(b.sem("h2"), r * NF + f - 2)
                    nc.scalar.activation(b.cv[:, f % 3], b.padded[:, f % 3, :, 1:S + 1], ACT.Identity, bias=conv[:, f, 3:4], scale=conv[:, f, 1:2]).then_inc(b.sem("mid"), 1)
                    if f:
                        silu(f - 1)
                silu(NF - 1)
                yield
                act.wait_ge(b.sem("s_ps"), 2 * r + 2)
                nc.scalar.activation(b.srow2[:], b.pD[:, 0:GT], ACT.Copy).then_inc(b.sem("srow"), 1)
                if b.number == 0:
                    load_exp_and_ln(nc)
                yield from layer_norm_scalar(nc, act, b.sem, "c", b.nb, r)
                yield
                act.wait_ge(b.sem("lT_ps"), 4 * r + 4)
                nc.scalar.activation(b.lT[:], dim(b.pB), ACT.Copy).then_inc(b.sem("lT"), 1)
                yield
                act.wait_ge(b.sem("q3_ps"), r + 1)
                act.wait_ge(b.sem("q3_out"), 16 * r)
                nc.scalar.activation(b.q3[:], dim(b.pC), ACT.Copy, scale=0.25).then_inc(b.sem("q3"), 1)

            with act.Fori(0, R) as r:
                in_turn(work, streams, r)
        @block.tensor
        def _(pe):
            pe.wait_ge(sem("const_in"), NL)
            pe.wait_ge(sem("set"), 1)
            pe.wait_ge(sem("wsum"), 1)
            nc.tensor.matmul(streams[0].pD[:, 0:2], ones[:], wsum[:], start=True, stop=True).then_inc(sem("wsum_ps"), 1)
            pe.wait_ge(sem("w2q"), 1)
            pe.wait_ge(sem("identb"), 1)
            def work(b, r):
                pe.wait_ge(b.sem("x_in"), 32 * (r + 1))
                pe.wait_ge(b.sem("x2"), r)
                by_token(nc, tok(b.pA), b.os_, wm["WoT0"]).then_inc(b.sem("y_ps"), 1)
                yield
                pe.wait_ge(b.sem("a_norm"), r + 1)
                pe.wait_ge(b.sem("lT"), 3 * r)
                transpose_group(nc, dim(b.pB), b.ln, ident).then_inc(b.sem("lT_ps"), 1)
                yield
                pe.wait_ge(b.sem("lT"), 3 * r + 1)
                pe.wait_ge(b.sem("q3"), r)
                by_dim(nc, dim(b.pC), b.lT, wm["Wq"]).then_inc(b.sem("q_ps"), 1)
                by_token(nc, tok(b.pD), b.lT, wm["Wk"]).then_inc(b.sem("k_ps"), 1)
                by_token(nc, tok(b.pA), b.lT, wm["Wv"]).then_inc(b.sem("v_ps"), 1)
                by_token(nc, tok(b.pB), b.lT, wm["Wg"]).then_inc(b.sem("g_ps"), 1)
                yield
                pe.wait_ge(b.sem("kp"), r + 1)
                pe.wait_ge(b.sem("qp"), r + 1)
                pe.wait_ge(b.sem("vb"), r + 1)
                for c in range(NBG):
                    h, t = 64 * (c % 2), c // 2
                    for o in range(2):
                        n = 2 * (c // 2) + o
                        i = nc.tensor.matmul((b.pD if c % 2 else b.pC)[:, 128 * n:128 * n + 128],
                                             b.kb[h:h + 64, t, 128 * o:128 * o + 128], b.vb[h:h + 64, t, 128 * o:128 * o + 128], start=True, stop=True)
                i.then_inc(b.sem("kv_ps"), 1)
                yield
                pe.wait_ge(b.sem("kvm"), r + 1)
                for c in range(NBG):
                    h, t = 64 * (c % 2), c // 2
                    for o in range(2):
                        i = nc.tensor.matmul(tok(b.pA)[h:h + 64, t, 128 * o:128 * o + 128], b.qp[:, o, S * c:S * c + S], b.kvm[:, NBG * (c % 2) + 2 * (c // 2) + o, :], start=True, stop=True)
                i.then_inc(b.sem("at_ps"), 1)
                yield
                pe.wait_ge(b.sem("gt"), r + 1)
                transpose_group(nc, dim(b.pB), b.gb, ident).then_inc(b.sem("lT_ps"), 1)
                yield
                pe.wait_ge(b.sem("lT"), 3 * r + 2)
                by_token(nc, tok(b.pC), b.lT, wm["Wo"]).then_inc(b.sem("o_ps"), 1)
                yield
                pe.wait_ge(b.sem("diag"), 2 * r + 1)
                for t in range(GROUP):
                    i = nc.tensor.matmul(b.pD[:, TOK * t:TOK * t + TOK], ones[:], b.diag[:, t, :], start=True, stop=True)
                i.then_inc(b.sem("s_ps"), 1)
                yield
                pe.wait_ge(b.sem("xq"), r + 1)
                transpose_group(nc, b.pA[:, 0:GT].bitcast(BF16).rearrange("p (k n) -> p k n", k=2), b.xq, identb).then_inc(b.sem("lT_ps"), 1)
                yield
                pe.wait_ge(b.sem("xqT"), r + 1)
                for f in range(NF):
                    yield
                    if f >= 3:
                        pe.wait_ge(b.sem("hs"), r * NF + f - 2)
                    for k in range(2):
                        i = nc.tensor.matmul(bank(b, f), w1q[:, k, 128 * f:128 * f + 128], b.xqT[:, k, :], start=k == 0, stop=k == 1)
                    i.then_inc(b.sem("h_ps"), 1)
                yield
                pe.wait_ge(b.sem("mx"), r + 1)
                pe.wait_ge(b.sem("srow"), 2 * r + 1)
                for t in range(GROUP):
                    i = nc.tensor.transpose(b.pD[:, GT + TOK * t:GT + TOK * t + TOK], b.mx[:, TOK * t:TOK * t + TOK], ident[:])
                i.then_inc(b.sem("mxT_ps"), 1)
                yield
                pe.wait_ge(b.sem("diag"), 2 * r + 2)
                for t in range(GROUP):
                    i = nc.tensor.matmul(b.pD[:, TOK * t:TOK * t + TOK], ones[:], b.diag[:, t, :], start=True, stop=True)
                i.then_inc(b.sem("s_ps"), 1)
                yield
                for f in range(NF):
                    if f % 2 == 0:
                        pe.wait_ge(b.sem("h2q"), r * (NF // 2) + f // 2 + 1)
                    for t in range(GROUP):
                        i = nc.tensor.matmul(tok(b.pA)[:, t, :], b.h2q[:, f, TOK * t:TOK * t + TOK], w2q[:, f, :],
                                             start=f == 0 and t == 0, stop=f == NF - 1, skip_group_check=True)
                i.then_inc(b.sem("y2_ps"), 1)
                yield
                pe.wait_ge(b.sem("c_norm"), r + 1)
                transpose_group(nc, dim(b.pB), b.ln, ident).then_inc(b.sem("lT_ps"), 1)
                yield
                pe.wait_ge(b.sem("lT"), 3 * r + 3)
                by_dim(nc, dim(b.pC), b.lT, wm["Wq3"]).then_inc(b.sem("q3_ps"), 1)

            with pe.Fori(0, R) as r:
                in_turn(work, streams, r)
        @block.vector
        def _(dve):
            v = nc.vector
            chain = Chain(dve, sem("dve"))

            dve.wait_ge(sem("wsum_ps"), 1)
            chain.step(v.tensor_scalar(wmean[:], streams[0].pD[:, 0:2], 1.0 / (1024 * 256), 1e-5, ALU.mult, ALU.max))
            chain.step(v.reciprocal(wscale[:], wmean[:]))
            for k, (w, wq) in enumerate(((w1, w1q), (w2, w2q))):
                flat = streams[0].h2[:].rearrange("p a b -> p (a b)")
                chain.step(v.tensor_scalar(flat, w[:].rearrange("p a b -> p (a b)"), wscale[:, k:k + 1], ROUND, ALU.mult, ALU.add))
                chain.step(v.tensor_scalar(flat, flat, ROUND, 1.0, ALU.subtract, ALU.min))
                i = v.tensor_scalar(wq[:].rearrange("p a b -> p (a b)"), flat, -1.0, None, ALU.max)
                if k == 0:
                    chain.step(i)
            i.then_inc(sem("w2q"), 1)
            dve.wait_ge(sem("w2q"), 1)
            dve.wait_ge(sem("set"), 1)
            dve.wait_ge(sem("const_in"), NL)
            PER = 45
            for b in streams:
                b.chain = Chain(dve, b.sem("dve"))
            def work(b, r):
                dve.wait_ge(b.sem("x_in"), 32 * (r + 1))
                dve.wait_ge(b.sem("y_ps"), r + 1)
                dve.wait_ge(b.sem("x2_out"), 16 * r)
                b.chain.step(v.tensor_tensor(b.x1[:], tok(b.pA), b.xs[:], ALU.add))
                b.chain.step(v.tensor_tensor(b.x1[:], b.x1[:], wide("bo0"), ALU.add))
                yield from layer_norm_vector(nc, b.chain, b.sem, "a", b.nb, b.x1, b.ln, r)
                yield
                dve.wait_ge(b.sem("q_ps"), r + 1)
                for o in range(2):
                    i = v.tensor_scalar(b.qp[:, o], dim(b.pC)[:, o], bq[:, o:o + 1], None, ALU.add)
                i.then_inc(b.sem("qb"), 1)
                yield
                dve.wait_ge(b.sem("k_ps"), r + 1)
                v.tensor_tensor(b.kb[:], tok(b.pD), wide("bk"), ALU.add).then_inc(b.sem("kb"), 1)
                yield
                dve.wait_ge(b.sem("v_ps"), r + 1)
                v.tensor_tensor(b.vb[:], tok(b.pA), wide("bv"), ALU.add).then_inc(b.sem("vb"), 1)
                yield
                dve.wait_ge(b.sem("qe"), r + 1)
                b.chain.step(v.tensor_scalar(b.qp[:], b.qp[:], 0.0, None, ALU.max))
                v.scalar_tensor_tensor(out=b.qp[:], in0=b.qe[:], scalar=1.0, in1=b.qp[:], op0=ALU.min, op1=ALU.add).then_inc(b.sem("qp"), 1)
                yield
                dve.wait_ge(b.sem("ke"), r + 1)
                b.chain.step(v.tensor_scalar(b.kb[:], b.kb[:], 0.0, None, ALU.max))
                v.scalar_tensor_tensor(out=b.kb[:], in0=b.ke[:], scalar=1.0, in1=b.kb[:], op0=ALU.min, op1=ALU.add).then_inc(b.sem("kp"), 1)
                yield
                dve.wait_ge(b.sem("g_ps"), r + 1)
                v.tensor_tensor(b.gb[:], tok(b.pB), wide("bg"), ALU.add).then_inc(b.sem("gb"), 1)
                yield
                dve.wait_ge(b.sem("kv_ps"), r + 1)
                hm = hmask[:].unsqueeze(1).to_broadcast([128, NBG, 128])
                v.tensor_tensor(b.kvm[:, 0:NBG], b.pC[:].rearrange("p (n e) -> p n e", n=NBG), hm, ALU.mult)
                v.tensor_tensor(b.kvm[:, NBG:], b.pD[:].rearrange("p (n e) -> p n e", n=NBG), hm, ALU.mult).then_inc(b.sem("kvm"), 1)
                yield
                dve.wait_ge(b.sem("at_ps"), r + 1)
                dve.wait_ge(b.sem("gs"), r + 1)
                v.tensor_tensor(b.gb[:], tok(b.pA), b.gb[:], ALU.mult).then_inc(b.sem("gt"), 1)
                yield
                dve.wait_ge(b.sem("o_ps"), r + 1)
                b.chain.step(v.tensor_tensor(b.x1[:], tok(b.pC), b.x1[:], ALU.add))
                b.chain.step(v.tensor_tensor(b.x1[:], b.x1[:], wide("bo"), ALU.add))
                yield from layer_norm_vector(nc, b.chain, b.sem, "b", b.nb, b.x1, b.ln, r)
                b.chain.step(v.tensor_reduce(b.am[:], b.ln[:], AX.X, ALU.max, apply_absolute_value=True))
                quantizing_scales(nc, b.chain, b.am[:], b.qs[:], b.s1[:], wmean[:, 0:1])
                for t in range(GROUP):
                    i = v.tensor_scalar(b.diag[:, t, :], ident[:], b.s1[:, t:t + 1], None, ALU.mult)
                i.then_inc(b.sem("diag"), 1)
                for t in range(GROUP):
                    i = v.tensor_scalar(b.ln[:, t, :], b.ln[:, t, :], b.qs[:, t:t + 1], ROUND, ALU.mult, ALU.add)
                b.chain.step(i)
                v.tensor_scalar(b.xq[:], b.ln[:], ROUND, None, ALU.subtract).then_inc(b.sem("xq"), 1)
                yield
                dve.wait_ge(b.sem("srow"), 2 * r + 1)
                for f in range(NF):
                    yield
                    dve.wait_ge(b.sem("h_ps"), r * NF + f + 1)
                    if f >= 3:
                        dve.wait_ge(b.sem("conv"), r * NF + f - 2)
                        dve.wait_ge(b.sem("mid"), r * NF + f - 2)
                    v.tensor_tensor(b.padded[:, f % 3, :, 1:S + 1], bank(b, f).rearrange("p (b s) -> p b s", s=S),
                                    b.srow[:].rearrange("p (b s) -> p b s", s=S), ALU.mult).then_inc(b.sem("hs"), 1)
                    yield
                    dve.wait_ge(b.sem("hs"), r * NF + f + 1)
                    dve.wait_ge(b.sem("mid"), r * NF + f + 1)
                    b.chain.step(v.scalar_tensor_tensor(out=b.cv[:, f % 3], in0=b.padded[:, f % 3, :, 0:S], scalar=conv[:, f, 0:1], in1=b.cv[:, f % 3], op0=ALU.mult, op1=ALU.add))
                    v.scalar_tensor_tensor(out=b.cv[:, f % 3], in0=b.padded[:, f % 3, :, 2:S + 2], scalar=conv[:, f, 2:3], in1=b.cv[:, f % 3], op0=ALU.mult, op1=ALU.add).then_inc(b.sem("conv"), 1)
                yield
                dve.wait_ge(b.sem("h2"), (r + 1) * NF)
                v.tensor_reduce(b.mx[:], b.h2[:].rearrange("p f t -> p t f"), AX.X, ALU.max, apply_absolute_value=True).then_inc(b.sem("mx"), 1)
                yield
                dve.wait_ge(b.sem("mxT_ps"), r + 1)
                b.chain.step(v.tensor_reduce(b.am2[:], b.pD[:, GT:2 * GT].rearrange("p (t n) -> p t n", t=GROUP), AX.X, ALU.max))
                quantizing_scales(nc, b.chain, b.am2[:], b.qs2[:], b.s2[:], wmean[:, 1:2])
                for t in range(GROUP):
                    i = v.tensor_scalar(b.diag[:, t, :], ident[:], b.qs2[:, t:t + 1], None, ALU.mult)
                i.then_inc(b.sem("diag"), 1)
                yield
                dve.wait_ge(b.sem("srow"), 2 * r + 2)
                for f in range(0, NF, 2):
                    b.chain.step(v.tensor_tensor(b.h2r[:, f:f + 2], b.h2[:, f:f + 2], b.srow2[:].unsqueeze(1).to_broadcast([128, 2, GT]), ALU.mult))
                    v.tensor_scalar(b.h2q[:, f:f + 2], b.h2r[:, f:f + 2], ROUND, ROUND, ALU.add, ALU.subtract).then_inc(b.sem("h2q"), 1)
                yield
                dve.wait_ge(b.sem("y2_ps"), r + 1)
                for t in range(GROUP):
                    i = v.scalar_tensor_tensor(out=b.x1[:, t, :], in0=tok(b.pA)[:, t, :], scalar=b.s2[:, t:t + 1], in1=b.x1[:, t, :], op0=ALU.mult, op1=ALU.add)
                i.then_inc(b.sem("x2"), 1)
                yield
                dve.wait_ge(b.sem("x2"), r + 1)
                yield from layer_norm_vector(nc, b.chain, b.sem, "c", b.nb, b.x1, b.ln, r)

            with dve.Fori(0, R) as r:
                for b in streams:
                    b.chain.enter(r, PER)
                in_turn(work, streams, r)
            for b in streams:
                b.chain.leave(R, PER)




def wide_cross_attention(nc, consts, ctxT, mask, Wkv, qT, oT):
    NB, DC, S2 = ctxT.shape
    H = DC // 2
    W2 = S2 + S2 % 2
    LAST = S2 - (NKT - 1) * KEYS
    L = qT.shape[1] // NB
    NP = 8
    NQ = 4
    with ExitStack() as ctx:
        m = Memory(nc, ctx, "xb")
        sem = m.sem
        ident = m.sbuf("ident", [128, 128])
        raw = m.sbuf("raw", [128, 2, W2])
        xst = m.sbuf("xst", [128, 3, 2, 4 * KEYS], F32R)
        w_raw = m.sbuf("w_raw", [128, 3, 512])
        whi = m.sbuf("whi", [128, 3, 512], F32R)
        wlo = m.sbuf("wlo", [128, 3, 512], F32R)
        kst = m.sbuf("kst", [128, 2, NQ, W2], F32R)
        val = m.sbuf("val", [128, 2, NKT, NP, 64])
        qf = m.sbuf("qf", [128, NQ, 4 * L])
        qhi = m.sbuf("qhi", [128, 2, NQ, 4 * L], F32R)
        qlo = m.sbuf("qlo", [128, 2, NQ, 4 * L], F32R)
        mask8 = m.sbuf("mask8", [128, W2], U8)
        some = m.sbuf("some", [128, 2])
        count = m.sbuf("count", [128, 1])
        mcopy = m.sbuf("mcopy", [128, W2], BF16)
        mbias = m.sbuf("mbias", [128, 2, W2], BF16)
        augk = m.sbuf("augk", [96, 2, W2], BF16)
        augq = m.sbuf("augq", [96, 1024], BF16)
        maxes = m.sbuf("maxes", [128, 2, NP, 4])
        negmax = m.sbuf("negmax", [128, NP, 33])
        junk = m.sbuf("junk", [128, 2, 4 * KEYS], BF16)
        P = m.sbuf("P", [128, 2, 1024])
        den = m.sbuf("den", [64, 512])
        o_sb = m.sbuf("o_sb", [64, 2, 512])
        ring = [m.psum(f"ring{k}", [128, 512]) for k in range(3)]
        sc = [m.psum(f"sc{k}", [128, 1024]) for k in range(2)]
        acc = m.psum("acc", [128, 512])

        ROUNDS = [("M", 0), ("S", 1), ("Q1", 0), ("V", 0), ("B", 0), ("A", 0), ("B", 1), ("A", 1), ("B", 2),
                  ("Q2", 0), ("A", 2), ("V", 1), ("A", 3), ("K", 1), ("S", 2), ("B", 3), ("A", 4), ("B", 4),
                  ("A", 5), ("K", 2), ("B", 5), ("A", 6), ("A", 7), ("S", 3), ("B", 6), ("V", 2), ("A", 8), ("B", 7),
                  ("A", 9), ("B", 8), ("A", 10), ("K", 3), ("B", 9), ("A", 11), ("Sn", 0), ("V", 3), ("Qn", 0),
                  ("A", 12), ("B", 10), ("A", 13), ("B", 11), ("A", 14), ("B", 12), ("A", 15), ("PVend", 0),
                  ("mred", 0), ("F0", 0), ("Kn", 0)]
        OF_B = ("M", "B", "PVend", "F0")
        FILLS = []
        for kind, c in [x for x in ROUNDS if x[0] == "Kn"] + ROUNDS:
            if kind == "Kn" and not FILLS:
                FILLS += [(("K", c, o), "klo", 8, 2 * c + o) for o in range(2)]
            elif kind == "K":
                FILLS += [((kind, c, o), "klo", 8, 2 * c + o) for o in range(2)]
            elif kind == "V":
                FILLS += [((kind, c, h), "val", 8, 2 * c + h) for h in range(2)]
            elif kind == "A":
                FILLS += [((kind, c, o), "maxed", 32, 2 * c + o) for o in range(2)]
        assert len(FILLS) % len(ring) == 0
        PLACE = {f[0]: n for n, f in enumerate(FILLS)}

        def schedule(engine_step, loop_engine, chain=None, per_round=0):
            def one(n, p, do_a, do_b, do_next):
                for kind, c in ROUNDS:
                    if kind in OF_B:
                        if do_b:
                            engine_step(kind, c, n, p)
                    elif kind in ("Qn", "Sn", "Kn"):
                        if do_next:
                            engine_step(kind[0], c, n + 2, p)
                    elif do_a:
                        engine_step(kind, c, n + 1, 1 - p)
            for kind in ("Q", "S", "K"):
                engine_step(kind, 0, 0, 0)
            one(-1, 1, True, False, True)
            with loop_engine.Fori(0, (NB - 2) // 2) as i:
                if chain:
                    chain.enter(i, per_round)
                one(i * 2, 0, True, True, True)
                one(i * 2 + 1, 1, True, True, True)
            if chain:
                chain.leave((NB - 2) // 2, per_round)
            one(NB - 2, 0, True, True, False)
            one(NB - 1, 1, False, True, False)

        def columns(c):
            t0, nt = CHUNKS[c]
            return t0 * KEYS, nt * KEYS if c < 3 else W2 - t0 * KEYS

        def pbuf(c, p):
            return (c + p) % 2

        def first(n, *more):
            return isinstance(n, int) and n == 0 and all(more)

        block = ctx.enter_context(nc.Block())

        @block.sync
        def _(sp):
            sp.dma_start(ident[:], consts["ident"]).then_inc(sem("const_in"), 16)
            for rows, k, dims in ((slice(0, 128), 0, slice(0, 128)), (slice(0, 64), 1, slice(128, 192)),
                                  (slice(64, 128), 1, slice(0, 64)), (slice(0, 128), 2, slice(64, 192))):
                sp.dma_start(w_raw[rows, k, :], Wkv[dims, :]).then_inc(sem("const_in"), 16)
            sp.wait_ge(sem("zeroed"), 1)

            def load_ctx(c, n):
                k0, w = columns(c)
                w = min(w, S2 - k0)
                for k, (d0, d1) in enumerate(((0, 128), (128, DC))):
                    sp.dma_start(raw[0:d1 - d0, k, k0:k0 + w],
                                 ctxT[bass.ds(n, 1), d0:d1, k0:k0 + w].rearrange("o p k -> p (o k)")).then_inc(sem(f"raw_in{c}"), 16)

            def load_small(n):
                sp.dma_start(mask8[:, 0:S2], mask[bass.ds(n, 1), :].rearrange("o k -> (o k)").partition_broadcast(128)).then_inc(sem("small_in"), 16)
                for h in range(4):
                    src = qT[:, bass.ds(n * L, L)].rearrange("(g h p) i -> h p g i", h=4, p=16)
                    for dup in range(2):
                        r = 64 * dup + 16 * h
                        sp.dma_start(qf[r:r + 16, :, L * h:L * h + L], src[h]).then_inc(sem("small_in"), 16)

            for c in range(4):
                load_ctx(c, 0)
            load_small(0)

            def step(kind, c, n, p):
                last = isinstance(n, int) and n + 1 >= NB
                if (kind, c > 0) in (("V", False), ("S", True)) and not last:
                    sp.wait_ge(sem("xlo"), nth(n, 4, c))
                    wait_apart(sp)
                    load_ctx(c, n + 1)
                if kind == "A" and c == 2 and not last:
                    sp.wait_ge(sem("qlo"), nth(n, 1, 0))
                    sp.wait_ge(sem("mbias"), nth(n, 1, 0))
                    wait_apart(sp)
                    load_small(n + 1)
                if kind == "F0":
                    sp.wait_ge(sem("o_sb"), nth(n, 1, 0))
                    dst = oT[:, bass.ds(n * L, L)].rearrange("(g q h d) i -> q h d g i", q=2, h=2, d=16)
                    for q in range(2):
                        for h in range(2):
                            r = 32 * q + 16 * h
                            src = o_sb[r:r + 16, p, :].rearrange("r (g h i) -> r g h i", g=4, h=2)[:, :, h, :]
                            sp.dma_start(dst[q, h], src).then_inc(sem(f"o_out{p}"), 16)
            schedule(step, sp)
            sp.wait_ge(sem("o_out0"), 32 * NB)
            sp.wait_ge(sem("o_out1"), 32 * NB)

        @block.gpsimd
        def _(pool):
            nc.gpsimd.memset(raw[:], 0.0)
            nc.gpsimd.memset(mask8[:], 0)
            nc.gpsimd.memset(qf[:], 0.0).then_inc(sem("zeroed"), 1)
            nc.gpsimd.memset(augk[:], 0.0)
            nc.gpsimd.memset(augq[:], 0.0)
            nc.gpsimd.memset(negmax[:], 0.0).then_inc(sem("set"), 1)
            pool.wait_ge(sem("set"), 1)
            nc.gpsimd.memset(augk[0:1, :, :], 1.0)
            nc.gpsimd.memset(augk[32:33, :, :], 1.0)
            nc.gpsimd.memset(augq[64:65, :], 1.0).then_inc(sem("set"), 1)
            pool.wait_ge(sem("set"), 2)
            nc.gpsimd.memset(val[:], 1.0).then_inc(sem("set"), 1)
            pool.wait_ge(sem("set"), 3)

            def step(kind, c, n, p):
                if kind == "Q":
                    pool.wait_ge(sem("counted"), nth(n, 1, 0))
                    wait_apart(pool)
                    nc.gpsimd.tensor_scalar(some[:, 0:1], count[:], 1.0, None, ALU.min)
                    nc.gpsimd.tensor_scalar(some[:, 1:2], count[:], 1.0, -MASKED, ALU.min, ALU.mult).then_inc(sem("some"), 1)
                    pool.wait_ge(sem("some"), nth(n, 1, 0))
                    if not (isinstance(n, int) and n < 2):
                        pool.wait_ge(sem("maxed"), (n - 1) * 32)
                    wait_apart(pool)
                    nc.gpsimd.tensor_scalar(mbias[:, p, :], mask8[:], -1.0, some[:, 1:2], ALU.add, ALU.mult).then_inc(sem("mbias"), 1)
            schedule(step, pool)

        @block.scalar
        def _(act):
            load_exp_and_ln(nc)
            act.wait_ge(sem("const_in"), 80)
            nc.scalar.activation(whi[:], w_raw[:], ACT.Copy).then_inc(sem("whi"), 1)
            act.wait_ge(sem("set"), 3)

            def step(kind, c, n, p):
                if kind == "S":
                    k0, w = columns(c)
                    act.wait_ge(sem(f"raw_in{c}"), (n + 1) * 32)
                    if not first(n, c < 2):
                        act.wait_ge(sem("v_ps"), nth(n, 8, 2 * (c - 2) + 1))
                    nc.scalar.activation(xst[:, 0, c % 2, 0:w], raw[:, 0, k0:k0 + w], ACT.Copy)
                    nc.scalar.activation(xst[0:64, 1, c % 2, 0:w], raw[0:64, 1, k0:k0 + w], ACT.Copy).then_inc(sem("xhi"), 1)
                if kind == "K":
                    k0, w = columns(c)
                    for o in range(2):
                        f = PLACE["K", c, o]
                        act.wait_ge(sem("k_ps"), nth(n, 8, 2 * c + o))
                        if o == 0 and c == 0 and not (isinstance(n, int) and n < 2):
                            act.wait_ge(sem("pv"), (n - 1) * NKT)
                        for u in range(2):
                            i = nc.scalar.activation(kst[0:64, p, 2 * o + u, k0:k0 + w], ring[f % 3][64 * u:64 * u + 64, 0:w], ACT.Copy)
                        i.then_inc(sem("khi"), 1)
                if kind == "Q":
                    act.wait_ge(sem("small_in"), (n + 1) * 9 * 16)
                    if not first(n):
                        act.wait_ge(sem("some"), n)
                    nc.scalar.activation(mcopy[:], mask8[:], ACT.Copy, accum_out=count[:]).then_inc(sem("counted"), 1)
                if kind == "M":
                    act.wait_ge(sem("m_ps"), nth(n, 1, 0))
                    if not first(n):
                        act.wait_ge(sem("s_ps"), n * NKT)
                    nc.scalar.activation(augq[0:33, :], sc[0][0:33, :], ACT.Copy).then_inc(sem("aughi"), 1)
                if kind == "Q1":
                    act.wait_ge(sem("some"), nth(n, 1, 0))
                    if not (isinstance(n, int) and n < 2):
                        act.wait_ge(sem("pv"), (n - 1) * NKT)
                    nc.scalar.activation(qhi[:, p], qf[:], ACT.Copy, scale=some[:, 0:1]).then_inc(sem("qhi"), 1)
                if kind == "V":
                    t0, nt = CHUNKS[c]
                    for h in range(2):
                        f = PLACE["V", c, h]
                        act.wait_ge(sem("v_ps"), nth(n, 8, 2 * c + h))
                        tiles = list(range(t0 + 2 * h, min(t0 + nt, t0 + 2 * h + 2)))
                        for k, t in enumerate(tiles):
                            w = KEYS if t < NKT - 1 else LAST
                            i = nc.scalar.activation(val[0:w, p, t, :, 0:32],
                                                     ring[f % 3][0:w, 256 * k:256 * k + 256].rearrange("p (a d) -> p a d", d=32), ACT.Copy)
                        i.then_inc(sem("val"), 1)
                if kind == "B":
                    w = KEYS if c < NKT - 1 else LAST
                    act.wait_ge(sem("s_ps"), nth(n, NKT, c))
                    if not first(n, c < 2):
                        act.wait_ge(sem("pv"), nth(n, NKT, max(c - 2, -1)))
                    nc.scalar.activation(P[0:w, pbuf(c, p), :], sc[(c + 1) % 2][0:w, :], ACT.Exp).then_inc(sem("exped"), 1)
                if kind == "F0":
                    act.wait_ge(sem("pv"), nth(n, NKT, NKT - 1))
                    if not first(n):
                        act.wait_ge(sem("o_sb"), n)
                    nc.scalar.activation(den[0:32, :], acc[32:64, :], ACT.Ln)
                    nc.scalar.activation(den[32:64, :], acc[96:128, :], ACT.Ln).then_inc(sem("lden"), 1)
                    act.wait_ge(sem("lden"), nth(n, 1, 0))
                    nc.scalar.activation(den[:], den[:], ACT.Exp, scale=-1.0).then_inc(sem("rden"), 1)
            schedule(step, act)

        @block.tensor
        def _(pe):
            pe.wait_ge(sem("const_in"), 80)
            pe.wait_ge(sem("wlo"), 1)

            def room(key, n):
                f = PLACE[key]
                _, name, per, k = FILLS[f - 3]
                if f >= 3:
                    pe.wait_ge(sem(name), nth(n, per, k))
                elif not first(n):
                    pe.wait_ge(sem(name), nth(n - 1, per, k))
                return ring[f % 3]

            def project(out, x, w, by_key):
                for k, (a, part) in enumerate(((0, whi), (0, wlo), (1, whi), (1, wlo), (2, whi))):
                    l, r = (xst[:, a, x[0], x[1]], part[:, a, w]) if by_key else (part[:, a, w], xst[:, a, x[0], x[1]])
                    i = nc.tensor.matmul(out, l, r, start=k == 0, stop=k == 4)
                return i

            def weigh(c, n, p):
                w = KEYS if c < NKT - 1 else LAST
                pe.wait_ge(sem("exped"), nth(n, NKT, c))
                if c == 0 and not first(n):
                    pe.wait_ge(sem("o_sb"), n)
                for a in range(NP):
                    q, g = a % 2, a // 2
                    i = nc.tensor.matmul(acc[64 * q:64 * q + 64, 128 * g:128 * g + 128], val[0:w, p, c, a, :],
                                         P[0:w, pbuf(c, p), 128 * a:128 * a + 128], start=c == 0 and a < 2, stop=c == NKT - 1, skip_group_check=True)
                i.then_inc(sem("pv"), 1)

            def step(kind, c, n, p):
                if kind == "K":
                    k0, w = columns(c)
                    pe.wait_ge(sem("xlo"), nth(n, 4, c))
                    for o in range(2):
                        bank = room((kind, c, o), n)
                        cols = slice(128 * o, 128 * o + 128)
                        i = project(bank[:, 0:w], (c % 2, slice(0, w)), cols, False)
                        i.then_inc(sem("k_ps"), 1)
                if kind == "V":
                    t0, nt = CHUNKS[c]
                    for h2 in range(2):
                        bank = room((kind, c, h2), n)
                        for k in range(min(2, nt - 2 * h2)):
                            t = t0 + 2 * h2 + k
                            w = KEYS if t < NKT - 1 else LAST
                            j = (t - t0) * KEYS
                            i = project(bank[0:w, 256 * k:256 * k + 256], (c % 2, slice(j, j + w)), slice(256, 512), True)
                        i.then_inc(sem("v_ps"), 1)
                if kind == "A":
                    k0, w = columns(c // 4)
                    if c % 4 == 0:
                        pe.wait_ge(sem("klo"), nth(n, 8, 2 * (c // 4) + 1))
                        pe.wait_ge(sem("qhi"), nth(n, 1, 0))
                    for k in range(2):
                        a = 2 * (c % 4) + k
                        bank = room((kind, c, k), n)
                        i = nc.tensor.matmul(bank[:, 0:w], qhi[:, p, a // 2, 128 * (a % 2):128 * (a % 2) + 128],
                                             kst[:, p, a // 2, k0:k0 + w], start=True, stop=True)
                        i.then_inc(sem("a_ps"), 1)
                if kind == "M":
                    pe.wait_ge(sem("negmax"), nth(n, 1, 0))
                    if not first(n):
                        pe.wait_ge(sem("exped"), n * NKT)
                    for a in range(NP):
                        i = nc.tensor.matmul(sc[0][0:33, 128 * a:128 * a + 128], negmax[:, a, :], ident[:], start=True, stop=True)
                    i.then_inc(sem("m_ps"), 1)
                if kind == "B":
                    s = sc[(c + 1) % 2]
                    w = KEYS if c < NKT - 1 else LAST
                    k0 = c * KEYS
                    if c == 0:
                        pe.wait_ge(sem("augq"), nth(n, 1, 0))
                        pe.wait_ge(sem("augk"), nth(n, 1, 0))
                        pe.wait_ge(sem("qlo"), nth(n, 1, 0))
                        pe.wait_ge(sem("klo"), nth(n, 8, 7))
                        pe.wait_ge(sem("val"), nth(n, 8, 7))
                        if not first(n):
                            pe.wait_ge(sem("exped"), nth(n - 1, NKT, NKT - 1))
                    elif c >= 2:
                        pe.wait_ge(sem("exped"), nth(n, NKT, c - 2))
                    for g in range(2):
                        nc.tensor.matmul(s[0:w, 512 * g:512 * g + 512], augk[0:65, p, k0:k0 + w], augq[0:65, 512 * g:512 * g + 512], start=True, stop=True)
                        for quad in (2 * g, 2 * g + 1):
                            for q in (qhi, qlo):
                                i = nc.tensor.matmul(s[0:w, 256 * quad:256 * quad + 256], kst[:, p, quad, k0:k0 + w], q[:, p, quad, :],
                                                     start=False, stop=True, skip_group_check=True)
                    i.then_inc(sem("s_ps"), 1)
                    if c > 0:
                        weigh(c - 1, n, p)
                if kind == "PVend":
                    weigh(NKT - 1, n, p)
            schedule(step, pe)

        @block.vector
        def _(dve):
            v = nc.vector
            chain = Chain(dve, sem("dve"))
            dve.wait_ge(sem("whi"), 1)
            v.tensor_tensor(wlo[:], w_raw[:], whi[:].bitcast(F32), ALU.subtract).then_inc(sem("wlo"), 1)
            dve.wait_ge(sem("set"), 3)

            def step(kind, c, n, p):
                if kind == "S":
                    k0, w = columns(c)
                    dve.wait_ge(sem("xhi"), nth(n, 4, c))
                    cols = slice(k0, k0 + w)
                    hi = [xst[:, k, c % 2, 0:w].bitcast(F32) for k in range(2)]
                    v.tensor_tensor(xst[64:128, 1, c % 2, 0:w], raw[0:64, 0, cols], hi[0][0:64], ALU.subtract)
                    v.tensor_tensor(xst[0:64, 2, c % 2, 0:w], raw[64:128, 0, cols], hi[0][64:128], ALU.subtract)
                    v.tensor_tensor(xst[64:128, 2, c % 2, 0:w], raw[0:64, 1, cols], hi[1][0:64], ALU.subtract).then_inc(sem("xlo"), 1)
                if kind == "K":
                    k0, w = columns(c)
                    for o in range(2):
                        f = PLACE["K", c, o]
                        dve.wait_ge(sem("khi"), nth(n, 8, 2 * c + o))
                        for u in range(2):
                            i = v.tensor_tensor(kst[64:128, p, 2 * o + u, k0:k0 + w], ring[f % 3][64 * u:64 * u + 64, 0:w],
                                                kst[0:64, p, 2 * o + u, k0:k0 + w].bitcast(F32), ALU.subtract)
                        i.then_inc(sem("klo"), 1)
                if kind == "Q2":
                    dve.wait_ge(sem("qhi"), nth(n, 1, 0))
                    v.scalar_tensor_tensor(out=qlo[:, p], in0=qf[:], scalar=some[:, 0:1], in1=qhi[:, p].bitcast(F32), op0=ALU.mult, op1=ALU.subtract).then_inc(sem("qlo"), 1)
                if kind == "A":
                    k0, w = columns(c // 4)
                    if c == 0:
                        dve.wait_ge(sem("mbias"), nth(n, 1, 0))
                        v.tensor_copy(augk[64:65, p, :], mbias[64:65, p, :]).then_inc(sem("augk"), 1)
                    for k in range(2):
                        f = PLACE["A", c, k]
                        dve.wait_ge(sem("a_ps"), nth(n, 32, 2 * c + k))
                        if not first(n, c == 0):
                            dve.wait_ge(sem("maxed"), nth(n, 32, 2 * c + k - 2))
                        wait_apart(chain.engine)
                        v.tensor_tensor_reduce(out=junk[:, k, 0:w], in0=ring[f % 3][:, 0:w], in1=mbias[:, p, k0:k0 + w],
                                               scale=1.0, scalar=-3.0e38, op0=ALU.add, op1=ALU.max,
                                               accum_out=maxes[:, p, 2 * (c % 4) + k, c // 4:c // 4 + 1]).then_inc(sem("maxed"), 1)
                if kind == "mred":
                    dve.wait_ge(sem("maxed"), nth(n, 32, 31))
                    if not first(n):
                        dve.wait_ge(sem("m_ps"), n)
                    for col in (0, 32):
                        i = v.tensor_reduce(negmax[:, :, col], maxes[:, p], AX.X, ALU.max)
                    chain.step(i)
                    for col in (0, 32):
                        i = v.tensor_scalar(negmax[:, :, col], negmax[:, :, col], -1.0, None, ALU.mult)
                    i.then_inc(sem("negmax"), 1)
                if kind == "M":
                    dve.wait_ge(sem("aughi"), nth(n, 1, 0))
                    v.tensor_tensor(augq[32:33, :], sc[0][32:33, :], augq[32:33, :], ALU.subtract).then_inc(sem("augq"), 1)
                if kind == "F0":
                    dve.wait_ge(sem("rden"), nth(n, 1, 0))
                    if not (isinstance(n, int) and n < 2):
                        dve.wait_ge(sem(f"o_out{p}"), 32 * n - 32 * p)
                    v.tensor_tensor(o_sb[0:32, p, :], acc[0:32, :], den[0:32, :], ALU.mult)
                    i = v.tensor_tensor(o_sb[32:64, p, :], acc[64:96, :], den[32:64, :], ALU.mult)
                    i.then_inc(sem("o_sb"), 1)
                    dve.wait_ge(sem("o_sb"), nth(n, 1, 0))
            schedule(step, dve, chain, 2)


ERF_P = (-2.72614225801306e-10, 2.77068142495902e-08, -2.10102402082508e-06, -5.69250639462346e-05,
         -7.34990630326855e-04, -2.95459980854025e-03, -1.60960333262415e-02)
ERF_Q = (-1.45660718464996e-05, -2.13374055278905e-04, -1.68282697438203e-03, -7.37332916720468e-03,
         -1.42647390514189e-02)
LAPLACE_MEAN = 0.5 ** 0.5
LAPLACE_WIDTH = (0.25 * np.pi) ** 0.5 * 2 ** 0.5


def laplacian_attention_and_router(nc, consts, x2, oT, W, x4, xn, logits, buf):
    N, D = x2.shape
    GT = GROUP * TOK
    S = 64
    R = N // (2 * GT)
    E = W["wg"].shape[1]
    with ExitStack() as ctx:
        m = Memory(nc, ctx, "la")
        sem = m.sem
        ident = m.sbuf("ident", [128, 128])
        half = m.sbuf("half", [128, 128])
        buckets = m.sbuf("buckets", [128, 32, S])
        rel = m.sbuf("rel", [128, 32])
        shift = m.sbuf("shift", [128, 128])
        wo = m.sbuf("wo", [128, 2, 256])
        wqk = m.sbuf("wqk", [128, 2, 128])
        wv = m.sbuf("wv", [128, 2, 256])
        wg = m.sbuf("wg", [128, 2, E])
        bqk = m.sbuf("bqk", [128, 1])
        gamma = m.sbuf("gamma", [128, 2])
        beta = m.sbuf("beta", [128, 2])
        bv = m.sbuf("bv", [128, 256])
        zeros = m.sbuf("zeros", [ROWS, 6 * 256])
        streams = [Stream(m, k) for k in range(2)]
        for b in streams:
            b.xs = b.sbuf("xs", [TOK, GROUP, 256])
            b.os_ = b.sbuf("os", [128, 2, GT])
            b.x3 = b.sbuf("x3", [TOK, GROUP, 256])
            b.l3 = b.sbuf("l3", [TOK, GROUP, 256])
            b.y4 = b.sbuf("y4", [TOK, GROUP, 256])
            b.l4 = b.sbuf("l4", [TOK, GROUP, 256])
            b.lT = b.sbuf("lT", [128, 2, GT])
            b.sqk = b.sbuf("sqk", [128, GT])
            b.qk = b.sbuf("qk", [128, 2, GT])
            b.vb = b.sbuf("vb", [TOK, GROUP, 256])
            b.vs = b.sbuf("vs", [TOK, GROUP, 256])
            b.z = b.sbuf("z", [128, GROUP, 128])
            b.z2 = b.sbuf("z2", [128, GROUP, 128])
            b.num = b.sbuf("num", [128, GROUP, 128])
            b.den = b.sbuf("den", [128, GROUP, 128])
            b.attn = b.sbuf("attn", [128, GROUP, 128])
            b.lg = b.sbuf("lg", [TOK, GROUP, E])
            b.nb = NormBuffers(b)
            b.pA, b.pB, b.pC, b.pD = (b.psum(f"p{k}", [128, 512]) for k in "ABCD")

        def tok(p):
            return p[:].rearrange("p (t n) -> p t n", t=GROUP)

        def dim(p):
            return p[:].rearrange("p (k n) -> p k n", k=2)

        def pairs(p, k):
            return p[:, GT * k:GT * k + GT].rearrange("p (t n) -> p t n", t=GROUP)

        def halves(w):
            return w.rearrange("(k p) n -> p k n", p=128)

        loads = [(ident[:], consts["ident"]), (half[:], consts["half"]), (buckets[:], consts["buckets"]), (rel[:], W["rel"].partition_broadcast(128)),
                 (wo[:], halves(W["Wo3"])), (wqk[:], halves(W["Wqk"])), (wv[:], halves(W["Wv4"])), (wg[:], halves(W["wg"])),
                 (bqk[:], W["bqk"]), (gamma[:], W["gamma"]), (beta[:], W["beta"]), (bv[:], W["bv4"].partition_broadcast(128))]
        NL = 16 * len(loads)

        block = ctx.enter_context(nc.Block())

        @block.sync
        def _(sp):
            for dst, src in loads:
                sp.dma_start(dst, src).then_inc(sem("const_in"), 16)
            def load(b, r):
                sp.dma_start(b.xs[:], tiles_of(x2, 2 * r + b.number)).then_inc(b.sem("x_in"), 16)
                sp.dma_start(b.os_[:], halves_of(oT, 2 * r + b.number)).then_inc(b.sem("x_in"), 16)

            def work(b, r, more):
                if more:
                    sp.wait_ge(b.sem("a_var"), r + 1)
                    wait_apart(sp)
                    load(b, r + 1)
                yield
                sp.wait_ge(b.sem("y4"), r + 1)
                wait_apart(sp)
                sp.dma_start(tiles_of(x4, 2 * r + b.number), b.y4[:]).then_inc(b.sem("out"), 16)
                yield
                sp.wait_ge(b.sem("b_norm"), r + 1)
                wait_apart(sp)
                sp.dma_start(tiles_of(xn, 2 * r + b.number), b.l4[:]).then_inc(b.sem("out"), 16)
                yield
                sp.wait_ge(b.sem("lg"), r + 1)
                wait_apart(sp)
                sp.dma_start(tiles_of(logits, 2 * r + b.number), b.lg[:]).then_inc(b.sem("out"), 16)
            for b in streams:
                load(b, 0)

            with sp.Fori(0, R - 1) as r:
                in_turn(work, streams, r, True)
            in_turn(work, streams, R - 1, False)
            for b in streams:
                sp.wait_ge(b.sem("out"), 48 * R)

        @block.gpsimd
        def _(pool):
            nc.gpsimd.memset(zeros[:], 0.0).then_inc(sem("zeros"), 1)
            pool.wait_ge(sem("zeros"), 1)
            pool.wait_ge(streams[0].sem("a_norm"), 1)
            slots = buf.rearrange("(a p t) n -> a p (t n)", p=ROWS, t=6)
            for a in range(buf.shape[0] // (6 * ROWS)):
                pool.dma_start(slots[a], zeros[:]).then_inc(sem("zeroed"), 16)
            pool.wait_ge(sem("zeroed"), 16 * (buf.shape[0] // (6 * ROWS)))

        @block.scalar
        def _(act):
            act.wait_ge(sem("const_in"), NL)
            def work(b, r):
                if b.number == 0:
                    load_exp_and_ln(nc)
                yield from layer_norm_scalar(nc, act, b.sem, "a", b.nb, r)
                yield
                act.wait_ge(b.sem("lT_ps"), 2 * r + 1)
                nc.scalar.activation(b.lT[:], dim(b.pB), ACT.Copy).then_inc(b.sem("lT"), 1)
                yield
                act.wait_ge(b.sem("qk_ps"), r + 1)
                act.wait_ge(b.sem("qk"), r)
                nc.scalar.activation(b.sqk[:], b.pC[:, 0:GT], ACT.Silu, bias=bqk[:]).then_inc(b.sem("sqk"), 1)
                yield
                act.wait_ge(b.sem("vb"), r + 1)
                nc.scalar.activation(b.vs[:], b.vb[:], ACT.Silu).then_inc(b.sem("vs"), 1)
                if b.number == 0:
                    load_exp_and_ln(nc)
                yield from layer_norm_scalar(nc, act, b.sem, "b", b.nb, r)
                yield
                act.wait_ge(b.sem("lT_ps"), 2 * r + 2)
                nc.scalar.activation(b.lT[:], dim(b.pB), ACT.Copy).then_inc(b.sem("lT"), 1)
                yield
                act.wait_ge(b.sem("lg_ps"), r + 1)
                act.wait_ge(b.sem("out"), 48 * r)
                nc.scalar.activation(b.lg[:], b.pD[:, 0:GROUP * E].rearrange("p (t e) -> p t e", e=E), ACT.Copy).then_inc(b.sem("lg"), 1)

            with act.Fori(0, R) as r:
                in_turn(work, streams, r)
        @block.tensor
        def _(pe):
            pe.wait_ge(sem("const_in"), NL)
            def work(b, r):
                pe.wait_ge(b.sem("x_in"), 32 * (r + 1))
                pe.wait_ge(b.sem("y4"), r)
                by_token(nc, tok(b.pA), b.os_, wo).then_inc(b.sem("y_ps"), 1)
                yield
                pe.wait_ge(b.sem("a_norm"), r + 1)
                pe.wait_ge(b.sem("lT"), 2 * r)
                transpose_group(nc, dim(b.pB), b.l3, ident).then_inc(b.sem("lT_ps"), 1)
                yield
                pe.wait_ge(b.sem("lT"), 2 * r + 1)
                pe.wait_ge(b.sem("lg"), r)
                pe.wait_ge(b.sem("z"), r)
                for k in range(2):
                    i = nc.tensor.matmul(b.pC[:, 0:GT], wqk[:, k, :], b.lT[:, k, :], start=k == 0, stop=k == 1)
                i.then_inc(b.sem("qk_ps"), 1)
                by_token(nc, tok(b.pD), b.lT, wv).then_inc(b.sem("v_ps"), 1)
                yield
                pe.wait_ge(b.sem("qk"), r + 1)
                for t in range(GROUP):
                    i = nc.tensor.matmul(pairs(b.pC, 1)[:, t, :], b.qk[:, 1, TOK * t:TOK * t + TOK], b.qk[:, 0, TOK * t:TOK * t + TOK], start=True, stop=True)
                i.then_inc(b.sem("sim_ps"), 1)
                yield
                pe.wait_ge(b.sem("attn"), r + 1)
                pe.wait_ge(b.sem("vs"), r + 1)
                for t in range(GROUP):
                    i = nc.tensor.matmul(tok(b.pA)[:, t, :], b.attn[:, t, :], b.vs[:, t, :], start=True, stop=True)
                i.then_inc(b.sem("o_ps"), 1)
                yield
                pe.wait_ge(b.sem("b_norm"), r + 1)
                transpose_group(nc, dim(b.pB), b.l4, ident).then_inc(b.sem("lT_ps"), 1)
                yield
                pe.wait_ge(b.sem("lT"), 2 * r + 2)
                by_token(nc, b.pD[:, 0:GROUP * E].rearrange("p (t e) -> p t e", e=E), b.lT, wg).then_inc(b.sem("lg_ps"), 1)

            with pe.Fori(0, R) as r:
                in_turn(work, streams, r)
        @block.vector
        def _(dve):
            v = nc.vector
            chain = Chain(dve, sem("dve"))
            dve.wait_ge(sem("const_in"), NL)
            chain.step(v.tensor_tensor(buckets[:], buckets[:], rel[:].unsqueeze(2).to_broadcast([128, 32, S]), ALU.mult))
            chain.step(v.tensor_reduce(shift[:, 0:S], buckets[:].rearrange("p k i -> p i k"), AX.X, ALU.add))
            for h in range(2):
                i = v.tensor_scalar(shift[:, S * (1 - h):S * (1 - h) + S], shift[:, 0:S], 128 ** 0.5 / LAPLACE_WIDTH, -LAPLACE_MEAN / LAPLACE_WIDTH, ALU.mult, ALU.add)
                chain.step(i)
            PER = 23
            for b in streams:
                b.chain = Chain(dve, b.sem("dve"))
            def work(b, r):
                dve.wait_ge(b.sem("x_in"), 32 * (r + 1))
                dve.wait_ge(b.sem("y_ps"), r + 1)
                b.chain.step(v.tensor_tensor(b.x3[:], tok(b.pA), b.xs[:], ALU.add))
                yield from layer_norm_vector(nc, b.chain, b.sem, "a", b.nb, b.x3, b.l3, r)
                yield
                dve.wait_ge(b.sem("sqk"), r + 1)
                for k in range(2):
                    i = v.tensor_scalar(b.qk[:, k, :], b.sqk[:], gamma[:, k:k + 1], beta[:, k:k + 1], ALU.mult, ALU.add)
                i.then_inc(b.sem("qk"), 1)
                yield
                dve.wait_ge(b.sem("v_ps"), r + 1)
                v.tensor_tensor(b.vb[:], tok(b.pD), bv[:].unsqueeze(1).to_broadcast([TOK, GROUP, 256]), ALU.add).then_inc(b.sem("vb"), 1)
                yield
                dve.wait_ge(b.sem("sim_ps"), r + 1)
                i = v.scalar_tensor_tensor(out=b.z[:], in0=pairs(b.pC, 1), scalar=1.0 / (S * LAPLACE_WIDTH), in1=shift[:].unsqueeze(1).to_broadcast([128, GROUP, 128]), op0=ALU.mult, op1=ALU.add)
                i.then_inc(b.sem("z"), 1)
                yield
                dve.wait_ge(b.sem("z"), r + 1)
                b.chain.step(v.tensor_scalar(b.z[:], b.z[:], 4.0, -4.0, ALU.min, ALU.max))
                b.chain.step(v.tensor_tensor(b.z2[:], b.z[:], b.z[:], ALU.mult))
                v.tensor_scalar(b.num[:], b.z2[:], ERF_P[0], None, ALU.mult)
                b.chain.step(v.tensor_scalar(b.den[:], b.z2[:], ERF_Q[0], None, ALU.mult))
                for k in range(1, 6):
                    i = v.scalar_tensor_tensor(out=b.num[:], in0=b.num[:], scalar=ERF_P[k], in1=b.z2[:], op0=ALU.add, op1=ALU.mult)
                    if k < 4:
                        i = v.scalar_tensor_tensor(out=b.den[:], in0=b.den[:], scalar=ERF_Q[k], in1=b.z2[:], op0=ALU.add, op1=ALU.mult)
                    if k == 4:
                        i = v.tensor_scalar(b.den[:], b.den[:], ERF_Q[4], None, ALU.add)
                    b.chain.step(i)
                v.scalar_tensor_tensor(out=b.num[:], in0=b.num[:], scalar=ERF_P[6], in1=b.z[:], op0=ALU.add, op1=ALU.mult)
                b.chain.step(v.reciprocal(b.den[:], b.den[:]))
                b.chain.step(v.tensor_tensor(b.num[:], b.num[:], b.den[:], ALU.mult))
                v.scalar_tensor_tensor(out=b.attn[:], in0=b.num[:], scalar=1.0, in1=half[:].unsqueeze(1).to_broadcast([128, GROUP, 128]), op0=ALU.add, op1=ALU.mult).then_inc(b.sem("attn"), 1)
                yield
                dve.wait_ge(b.sem("o_ps"), r + 1)
                dve.wait_ge(b.sem("out"), 48 * r)
                v.tensor_tensor(b.y4[:], tok(b.pA), b.x3[:], ALU.add).then_inc(b.sem("y4"), 1)
                yield
                dve.wait_ge(b.sem("y4"), r + 1)
                yield from layer_norm_vector(nc, b.chain, b.sem, "b", b.nb, b.y4, b.l4, r)

            with dve.Fori(0, R) as r:
                for b in streams:
                    b.chain.enter(r, PER)
                in_turn(work, streams, r)
            for b in streams:
                b.chain.leave(R, PER)


def routed_experts(nc, consts, x4, xn, logits, W, buf, ybuf, out):
    N, D = x4.shape
    E, _, F = W["W1"].shape
    NT = N // TOK
    NFT = F // 128
    CAP = int(N / E * 1.25) + 1
    SLOTS = E * CAP
    TE = CAP // ROWS
    FAR = 100000.0
    assert TE * ROWS == CAP
    with ExitStack() as ctx:
        m = Memory(nc, ctx, "ex")
        sem = m.sem
        ident = m.sbuf("ident", [128, 128])
        upto = m.sbuf("upto", [128, 128])
        ones = m.sbuf("ones", [128, 128])
        order = m.sbuf("order", [128, E])
        xs = m.sbuf("xs", [TOK, NT, D])
        x4s = m.sbuf("x4s", [TOK, NT, D])
        lg = m.sbuf("lg", [TOK, NT, E])
        ex = m.sbuf("ex", [TOK, NT, E])
        eq = m.sbuf("eq", [TOK, NT, E])
        oh = m.sbuf("oh", [TOK, NT, E])
        counts = m.sbuf("counts", [TOK, NT, E])
        run = m.sbuf("run", [TOK, 2, NT, E])
        mx = m.sbuf("mx", [TOK, NT])
        first = m.sbuf("first", [TOK, NT])
        weight = m.sbuf("weight", [TOK, NT])
        rank = m.sbuf("rank", [TOK, NT])
        room = m.sbuf("room", [TOK, NT])
        slot = m.sbuf("slot", [TOK, NT])
        far = m.sbuf("far", [TOK, NT])
        put = m.sbuf("put", [TOK, NT], U32)
        get = m.sbuf("get", [TOK, NT], U32)
        w1 = m.sbuf("w1", [128, 2, 2, F])
        w2 = m.sbuf("w2", [128, 2, NFT, D])
        b1 = m.sbuf("b1", [128, E, NFT])
        b2 = m.sbuf("b2", [128, 2, D])
        xe = m.sbuf("xe", [ROWS, 2, TE, D])
        xeT = m.sbuf("xeT", [128, 2, 2, CAP])
        hT = m.sbuf("hT", [128, NFT, CAP])
        ye = m.sbuf("ye", [ROWS, 2, TE, D])
        pX = m.psum("pX", [128, 2, 512])
        pH = m.psum("pH", [128, 4, 512])
        pY = m.psum("pY", [128, 2, 512])
        BY_EXPERT = 16 * 4

        def rows_of(b, e):
            return b[bass.ds(e * CAP, CAP), :].rearrange("(p t) n -> p t n", t=TE)

        def weights_in(sp, e, par):
            sp.dma_start(w1[:, par], W["W1"][bass.ds(e, 1), :, :].rearrange("a (k p) n -> p (a k) n", p=128)).then_inc(sem(f"w_in{par}"), 16)
            sp.dma_start(w2[:, par], W["W2"][bass.ds(e, 1), :, :].rearrange("a (k p) n -> p (a k) n", p=128)).then_inc(sem(f"w_in{par}"), 16)
            sp.dma_start(b2[:, par], W["b2"][bass.ds(e, 1), :].rearrange("a n -> (a n)").partition_broadcast(128)).then_inc(sem(f"w_in{par}"), 16)

        block = ctx.enter_context(nc.Block())

        @block.sync
        def _(sp):
            sp.dma_start(lg[:], logits.rearrange("(t p) e -> p t e", p=TOK)).then_inc(sem("lg_in"), 16)
            for dst, src in ((ident[:], consts["ident"]), (upto[:], consts["upto"]), (order[:], consts["order"]), (b1[:], W["b1"])):
                sp.dma_start(dst, src).then_inc(sem("const_in"), 16)
            sp.dma_start(xs[:], xn.rearrange("(t p) n -> p t n", p=TOK)).then_inc(sem("xs_in"), 16)
            for e in range(2):
                weights_in(sp, e, e)
            sp.dma_start(x4s[:], x4.rearrange("(t p) n -> p t n", p=TOK)).then_inc(sem("x4_in"), 16)
            sp.wait_ge(sem("put"), 16 * NT)
            for e in range(2):
                sp.dma_start(xe[:, e], rows_of(buf, e)).then_inc(sem(f"xe_in{e}"), 16)

            def expert(i, par, more):
                e = 2 * i + par
                if more:
                    sp.wait_ge(sem("xT_ps"), e + 1)
                    sp.dma_start(xe[:, par], rows_of(buf, e + 2)).then_inc(sem(f"xe_in{par}"), 16)
                sp.wait_ge(sem("ye"), e + 1)
                sp.dma_start(rows_of(ybuf, e), ye[:, par]).then_inc(sem(f"ye_out{par}"), 16)
                if more:
                    weights_in(sp, e + 2, par)
            with sp.Fori(0, E // 2 - 1) as i:
                expert(i, 0, True)
                expert(i, 1, True)
            expert(E // 2 - 1, 0, False)
            expert(E // 2 - 1, 1, False)
            for t in range(0, NT, 4):
                sp.wait_ge(sem("mix"), t // 4 + 1)
                sp.dma_start(out[TOK * t:TOK * t + 4 * TOK, :].rearrange("(t p) n -> p t n", p=TOK), x4s[:, t:t + 4]).then_inc(sem("out"), 16)
            sp.wait_ge(sem("out"), 16 * (NT // 4))

        @block.scalar
        def _(act):
            act.wait_ge(sem("shifted"), 1)
            nc.scalar.activation(ex[:], ex[:], ACT.Exp).then_inc(sem("exp"), 1)
            act.wait_ge(sem("const_in"), 64)

            def expert(e, par):
                act.wait_ge(sem("xT_ps"), e + 1)
                nc.scalar.activation(xeT[:, par], pX[:, :, 0:CAP], ACT.Copy).then_inc(sem("xT"), 1)
                if e:
                    act.wait_ge(sem("y_ps"), e)
                for f in range(NFT):
                    act.wait_ge(sem("h_ps"), e * NFT + f + 1)
                    nc.scalar.activation(hT[:, f, :], pH[:, f % 4, 0:CAP], ACT.Gelu, bias=b1[:, bass.ds(e, 1), f:f + 1].rearrange("p a b -> p (a b)")).then_inc(sem("h"), 1)
            for e in range(E):
                expert(e, e % 2)

        @block.tensor
        def _(pe):
            pe.wait_ge(sem("const_in"), 64)
            pe.wait_ge(sem("oh"), 1)
            pe.wait_ge(sem("set"), 1)
            flat = oh[:].rearrange("p t e -> p (t e)")
            nc.tensor.matmul(pH[:, 0, 0:NT * E], ones[:], flat, start=True, stop=True)
            nc.tensor.matmul(pH[:, 1, 0:NT * E], upto[:], flat, start=True, stop=True).then_inc(sem("rank_ps"), 1)
            pe.wait_ge(sem("ranked"), 1)

            def expert(i, par):
                e = 2 * i + par
                pe.wait_ge(sem(f"xe_in{par}"), 16 * (i + 1))
                for k in range(2):
                    for t in range(TE):
                        o = nc.tensor.transpose(pX[:, k, ROWS * t:ROWS * t + ROWS], xe[:, par, t, 128 * k:128 * k + 128], ident[0:ROWS, 0:ROWS])
                o.then_inc(sem("xT_ps"), 1)
                pe.wait_ge(sem("xT"), e + 1)
                pe.wait_ge(sem(f"w_in{par}"), 48 * (i + 1))
                for f in range(NFT):
                    if f >= 4:
                        pe.wait_ge(sem("h"), e * NFT + f - 3)
                    for k in range(2):
                        o = nc.tensor.matmul(pH[:, f % 4, 0:CAP], w1[:, par, k, 128 * f:128 * f + 128], xeT[:, par, k, :], start=k == 0, stop=k == 1)
                    o.then_inc(sem("h_ps"), 1)
                pe.wait_ge(sem("h"), (e + 1) * NFT)
                pe.wait_ge(sem("ye"), e)
                for t in range(TE):
                    for f in range(NFT):
                        o = nc.tensor.matmul(pY[0:ROWS, t // 2, 256 * (t % 2):256 * (t % 2) + 256], hT[:, f, ROWS * t:ROWS * t + ROWS], w2[:, par, f, :], start=f == 0, stop=f == NFT - 1)
                o.then_inc(sem("y_ps"), 1)
            with pe.Fori(0, E // 2) as i:
                expert(i, 0)
                expert(i, 1)

        @block.gpsimd
        def _(pool):
            nc.gpsimd.memset(ones[:], 1.0).then_inc(sem("set"), 1)
            pool.wait_ge(sem("xs_in"), 16)
            pool.wait_ge(sem("slots"), 1)
            for t in range(NT):
                pool.indirect_dma_start(buf, bass.IndirectOffsetOnAxis(put[:, t:t + 1], 0), xs[:, t, :], None,
                                        bounds_check=SLOTS - 1, oob_is_err=False).then_inc(sem("put"), 16)
            pool.wait_ge(sem("put"), 16 * NT)
            for par in range(2):
                pool.wait_ge(sem(f"ye_out{par}"), 8 * E)
            for t in range(NT):
                pool.indirect_dma_start(xs[:, t, :], None, ybuf, bass.IndirectOffsetOnAxis(get[:, t:t + 1], 0),
                                        bounds_check=SLOTS - 1, oob_is_err=False).then_inc(sem(f"got{t // 4}"), 16)

        @block.vector
        def _(dve):
            v = nc.vector
            chain = Chain(dve, sem("dve"))

            def wide(a):
                return a.unsqueeze(2).to_broadcast([TOK, NT, E])

            dve.wait_ge(sem("lg_in"), 16)
            chain.step(v.tensor_reduce(mx[:], lg[:], AX.X, ALU.max))
            v.tensor_tensor(ex[:], lg[:], wide(mx[:]), ALU.subtract).then_inc(sem("shifted"), 1)
            v.tensor_tensor(eq[:], lg[:], wide(mx[:]), ALU.is_ge).then_inc(sem("eq"), 1)
            dve.wait_ge(sem("eq"), 1)
            dve.wait_ge(sem("const_in"), 64)
            chain.step(v.tensor_tensor(eq[:], eq[:], order[:].unsqueeze(1).to_broadcast([TOK, NT, E]), ALU.mult))
            chain.step(v.tensor_reduce(first[:], eq[:], AX.X, ALU.max))
            v.tensor_tensor(oh[:], eq[:], wide(first[:]), ALU.is_equal).then_inc(sem("oh"), 1)
            dve.wait_ge(sem("exp"), 1)
            chain.step(v.tensor_reduce(weight[:], ex[:], AX.X, ALU.add))
            chain.step(v.reciprocal(weight[:], weight[:]))
            dve.wait_ge(sem("rank_ps"), 1)
            dve.wait_ge(sem("oh"), 1)
            by_tile = pH[:, 0, 0:NT * E].rearrange("p (t e) -> p t e", e=E)
            v.tensor_copy(counts[:], by_tile)
            chain.step(v.tensor_copy(run[:, 0], by_tile))
            for s in range(4):
                a, b, d = run[:, s % 2], run[:, (s + 1) % 2], 1 << s
                v.tensor_copy(b[:, 0:d], a[:, 0:d])
                chain.step(v.tensor_tensor(b[:, d:], a[:, d:], a[:, 0:NT - d], ALU.add))
            chain.step(v.tensor_tensor(run[:, 0], run[:, 0], counts[:], ALU.subtract))
            chain.step(v.tensor_tensor(run[:, 0], run[:, 0], pH[:, 1, 0:NT * E].rearrange("p (t e) -> p t e", e=E), ALU.add))
            chain.step(v.tensor_tensor(run[:, 0], run[:, 0], oh[:], ALU.mult))
            chain.step(v.tensor_reduce(rank[:], run[:, 0], AX.X, ALU.add))
            v.tensor_scalar(room[:], rank[:], CAP + 0.5, None, ALU.is_le)
            v.tensor_scalar(far[:], rank[:], CAP + 0.5, FAR, ALU.is_gt, ALU.mult)
            chain.step(v.scalar_tensor_tensor(out=slot[:], in0=first[:], scalar=-float(CAP), in1=rank[:], op0=ALU.mult, op1=ALU.add))
            chain.step(v.tensor_scalar(slot[:], slot[:], float(SLOTS - 1), None, ALU.add))
            chain.step(v.tensor_scalar(get[:], slot[:], float(SLOTS - 1), None, ALU.min))
            chain.step(v.tensor_tensor(weight[:], weight[:], room[:], ALU.mult))
            v.tensor_tensor(put[:], slot[:], far[:], ALU.add).then_inc(sem("slots"), 1)
            dve.wait_ge(sem("slots"), 1)
            v.tensor_copy(first[:], rank[:]).then_inc(sem("ranked"), 1)
            dve.wait_ge(sem("ranked"), 1)

            def expert(i, par, warm):
                e = 2 * i + par
                dve.wait_ge(sem("y_ps"), e + 1)
                dve.wait_ge(sem(f"w_in{par}"), 48 * (i + 1))
                if warm:
                    dve.wait_ge(sem(f"ye_out{par}"), 16 * i)
                v.tensor_tensor(ye[:, par, 0:2], pY[0:ROWS, 0, :].rearrange("p (t n) -> p t n", n=D), b2[0:ROWS, par].unsqueeze(1).to_broadcast([ROWS, 2, D]), ALU.add)
                v.tensor_tensor(ye[:, par, 2], pY[0:ROWS, 1, 0:D], b2[0:ROWS, par], ALU.add).then_inc(sem("ye"), 1)
            expert(0, 0, False)
            expert(0, 1, False)
            with dve.Fori(1, E // 2) as i:
                expert(i, 0, True)
                expert(i, 1, True)
            dve.wait_ge(sem("x4_in"), 16)
            for t in range(NT):
                if t % 4 == 0:
                    dve.wait_ge(sem(f"got{t // 4}"), 64)
                i = v.scalar_tensor_tensor(out=x4s[:, t, :], in0=xs[:, t, :], scalar=weight[:, t:t + 1], in1=x4s[:, t, :], op0=ALU.mult, op1=ALU.add)
                if t % 4 == 3:
                    i.then_inc(sem("mix"), 1)




def relative_buckets(seq_len, buckets=32, max_distance=128):
    at = np.arange(seq_len)
    n = np.maximum(at[:, None] - at[None, :], 0)
    exact = buckets // 2
    nf = np.maximum(n, 1).astype(np.float32)
    far = exact + (np.log(nf / exact) / np.log(max_distance / exact) * (buckets - exact)).astype(np.int32)
    return np.where(n < exact, n, np.minimum(far, buckets - 1))


def shape_constants(latents=64, experts=8, buckets=32):
    i = np.arange(128)
    bucket = relative_buckets(latents, buckets)
    onehot = (np.arange(buckets)[:, None, None] == bucket[None]).astype(np.float32)
    causal = (i[:, None] // latents == i[None] // latents) & (i[None] >= i[:, None])
    return {
        "ident": np.eye(128, dtype=np.float32),
        "head16": (i[:, None] // 16 == i[None] // 16).astype(np.float32),
        "half": np.where(causal, np.float32(0.5), np.float32(0)),
        "buckets": np.tile(onehot, (1, 1, 2)).transpose(2, 0, 1),
        "upto": (i[:, None] <= i[None]).astype(np.float32),
        "order": np.tile(experts - np.arange(experts, dtype=np.float32), (128, 1)),
    }


def perceiver(nc, a, out):
    N, D = a["x"].shape
    E = a["wg"].shape[1]
    slots = E * (int(N / E * 1.25) + 1)

    def scratch(name, shape):
        return nc.dram_tensor(name, shape, F32, kind="Internal").ap()
    qT, klT, oT0, q3T, oT3 = (scratch(name, (D, N)) for name in ("qT", "klT", "oT0", "q3T", "oT3"))
    vl, x2, x4, xn = (scratch(name, (N, D)) for name in ("vl", "x2", "x4", "xn"))
    logits = scratch("logits", (N, E))
    buf, ybuf = scratch("buf", (slots, D)), scratch("ybuf", (slots, D))

    latent_projections(nc, a, a["x"], a["ln_l_g"], a["ln_l_b"], a["qn_g"], a["kn_g"], a["WqT"], a["WlkvT"], qT, klT, vl)
    latent_cross_attention(nc, a, a["ctx"], a["mask0"], a["ln_x_g"], a["ln_x_b"], a["WkvT"], qT, klT, vl, oT0)
    gated_attention_and_ffn(nc, a, a["x"], oT0, a, x2, q3T)
    wide_cross_attention(nc, a, a["ctxT"], a["mask1"], a["Wkv3"], q3T, oT3)
    laplacian_attention_and_router(nc, a, x2, oT3, a, x4, xn, logits, buf)
    routed_experts(nc, a, x4, xn, logits, a, buf, ybuf, out)


def layout(i):
    x, ctx = i["x"], i["ctx_768"]
    B, S, D = x.shape
    F = i["L0_ffn_w1"].shape[0]
    E = i["L1_ffn_b1"].shape[0]

    def halves(v):
        return v.reshape(2, -1).T
    taps = np.concatenate([i["L0_ffn_conv_w"].reshape(F, 3), i["L0_ffn_conv_b"].reshape(F, 1)], 1)
    a = {
        "x": x.reshape(B * S, D), "ctx": ctx, "ctxT": ctx.transpose(0, 2, 1),
        "mask0": i["mask_BxS2_bk0"], "mask1": i["mask_BxS2_bf1"],
        "ln_x_g": halves(i["L0_xattn_ln_x_g"]), "ln_x_b": halves(i["L0_xattn_ln_x_b"]),
        "ln_l_g": i["L0_xattn_ln_l_g"], "ln_l_b": i["L0_xattn_ln_l_b"], "qn_g": i["L0_xattn_qn_g"], "kn_g": i["L0_xattn_kn_g"],
        "WqT": i["L0_xattn_Wq"].T, "WkvT": i["L0_xattn_Wkv"].T, "WlkvT": i["L0_xattn_Wlkv"].T,
        "WoT0": i["L0_xattn_Wo"].T, "bo0": i["L0_xattn_bo"],
        "Wq": i["L0_attn_Wq"], "bq": halves(i["L0_attn_bq"]), "Wk": i["L0_attn_Wk"], "bk": i["L0_attn_bk"],
        "Wv": i["L0_attn_Wv"], "bv": i["L0_attn_bv"], "Wg": i["L0_attn_Wg"], "bg": i["L0_attn_bg"],
        "Wo": i["L0_attn_Wo"], "bo": i["L0_attn_bo"],
        "w1T": i["L0_ffn_w1"].T, "w2T": i["L0_ffn_w2"].T, "conv": taps.reshape(F // 128, 128, 4).transpose(1, 0, 2),
        "Wq3": i["L1_xattn_Wq"], "Wkv3": np.concatenate([i["L1_xattn_Wk"], i["L1_xattn_Wv"]], 1), "Wo3": i["L1_xattn_Wo"],
        "Wqk": i["L1_attn_Wqk"], "bqk": i["L1_attn_bqk"].reshape(128, 1), "gamma": i["L1_attn_gamma"].T, "beta": i["L1_attn_beta"].T,
        "Wv4": i["L1_attn_Wv"], "bv4": i["L1_attn_bv"], "rel": i["L1_attn_rel_emb"].reshape(-1),
        "wg": i["L1_ffn_wg"], "W1": i["L1_ffn_W1"], "b1": i["L1_ffn_b1"].reshape(E, F // 128, 128).transpose(2, 0, 1),
        "W2": i["L1_ffn_W2"], "b2": i["L1_ffn_b2"],
    }
    a.update(shape_constants(S, E))
    return a


def kernel(**inputs):
    import concourse.bacc as bacc
    from concourse.bass_utils import run_bass_kernel_spmd

    given = {name: np.asarray(v) for name, v in inputs.items()}
    B, S, D = given["x"].shape
    arrays = {f"in_{name}": np.ascontiguousarray(v) for name, v in layout(given).items()}
    nc = bacc.Bacc("TRN2", target_bir_lowering=False, num_devices=1)
    a = {name[3:]: nc.dram_tensor(name, v.shape, mybir.dt.from_np(v.dtype), kind="ExternalInput").ap() for name, v in arrays.items()}
    out = nc.dram_tensor("out", (B * S, D), F32, kind="ExternalOutput").ap()
    perceiver(nc, a, out)
    r = run_bass_kernel_spmd(nc, [arrays], core_ids=[0])
    return r.results[0]["out"].reshape(B, S, D)
```
